# Optimizing a Trainium2 kernel written in Bass

```python
import numpy as np
import jax
import jax.numpy as jnp

def _softmax(x, axis=-1):
    return jax.nn.softmax(x, axis=axis)

def _gelu(x):
    return jax.nn.gelu(x, approximate=True)

def _silu(x):
    return jax.nn.silu(x)

def _sigmoid(x):
    return jax.nn.sigmoid(x)

def _layernorm(x, axis=-1, eps=1e-05):
    m = jnp.mean(x, axis=axis, keepdims=True)
    v = jnp.var(x, axis=axis, keepdims=True)
    return (x - m) / jnp.sqrt(v + eps)

def _scatter_add(tgt, idx, src, axis=0):
    return tgt.at[idx].add(src)

def _segment_sum(src, seg, n):
    return jax.ops.segment_sum(src, seg, n)
kernel_name = 'mk_gnn_preln_d2_gnn_r64_5bf964'

def setup_inputs(seed: int=0):
    np.random.seed(seed)
    _w = jnp.asarray

    def _rec_inputs():
        import jax
        import jax.numpy as jnp
        _gk = jax.random.key(seed)
        x = -0.000202 + 1 * jax.random.normal(jax.random.fold_in(_gk, 1), (100000, 128), jnp.float32)
        src = jax.random.randint(jax.random.fold_in(_gk, 2), (25000,), 0, 100000, jnp.int32)
        dst = jax.random.randint(jax.random.fold_in(_gk, 3), (25000,), 0, 100000, jnp.int32)
        _o = jnp.argsort(dst, stable=True)
        src = src[_o]
        dst = dst[_o]
        edge_attr_128 = 2.93046e-05 + 1.00006 * jax.random.normal(jax.random.fold_in(_gk, 12), (25000, 128), jnp.float32)
        edge_weight1 = 0.000452788 + 0.999756 * jax.random.normal(jax.random.fold_in(_gk, 15), (25000, 1), jnp.float32)
        return (x, src, dst, edge_attr_128, edge_weight1)
    x, src, dst, edge_attr_128, edge_weight1 = _rec_inputs()

    def _L0_gnn_setup():
        import jax, jax.numpy as jnp
        import numpy as np
        N_NODES = 50000
        N_EDGES = 10000
        C = 128
        BN_EPS = 0.0001

        def elu(x):
            return jnp.where(x > 0, x, jnp.expm1(x))

        def batchnorm_train(x, gamma, beta):
            mean = jnp.mean(x, axis=0)
            var = jnp.mean((x - mean) ** 2, axis=0)
            return gamma * (x - mean) * jax.lax.rsqrt(var + BN_EPS) + beta
        key = jax.random.key(seed)
        ks = jax.random.split(key, 8)
        x = jax.random.normal(ks[0], (N_NODES, C), dtype=jnp.float32)
        edge_index = jax.random.randint(ks[1], (2, N_EDGES), 0, N_NODES, dtype=jnp.int32)
        edge_attr = jax.random.normal(ks[2], (N_EDGES, C), dtype=jnp.float32)
        u = jax.random.normal(ks[3], (1, C), dtype=jnp.float32)
        batch = jnp.zeros((N_NODES,), dtype=jnp.int32)
        s1 = 1.0 / np.sqrt(2 * C)
        W1 = jax.random.uniform(ks[4], (2 * C, C), jnp.float32, -s1, s1)
        b1 = jnp.zeros((C,), jnp.float32)
        g1 = jnp.ones((C,), jnp.float32)
        be1 = jnp.zeros((C,), jnp.float32)
        W2 = jax.random.uniform(ks[5], (2 * C, C), jnp.float32, -s1, s1)
        b2 = jnp.zeros((C,), jnp.float32)
        g2 = jnp.ones((C,), jnp.float32)
        be2 = jnp.zeros((C,), jnp.float32)
        return dict(x=x, edge_index=edge_index, edge_attr=edge_attr, u=u, batch=batch, W1=W1, b1=b1, g1=g1, be1=be1, W2=W2, b2=b2, g2=g2, be2=be2)
    _L0_gnn_all = _L0_gnn_setup()
    _L0_gnn_in = {k: v for k, v in _L0_gnn_all.items() if k in ('u', 'W1', 'b1', 'g1', 'be1', 'W2', 'b2', 'g2', 'be2')}
    del _L0_gnn_all

    def _L1_gnn_setup():
        import jax, jax.numpy as jnp
        import numpy as np
        import math
        N = 100000
        E = 25000
        D = 128
        H = 8
        HD = D // H
        EPS = 1e-16

        def _xavier(key, shape):
            fan_out, fan_in = shape
            lim = math.sqrt(6.0 / (fan_in + fan_out))
            return jax.random.uniform(key, shape, jnp.float32, -lim, lim)
        key = jax.random.key(seed)
        ks = jax.random.split(key, 8)
        return {'feats': jax.random.normal(ks[0], (N, D), jnp.float32), 'edge_index': jax.random.randint(ks[1], (E, 2), 0, N, dtype=jnp.int64), 'edge_attr': jax.random.normal(ks[2], (E, 1), jnp.float32), 'Wq': _xavier(ks[3], (D, D)), 'bq': jnp.zeros((D,), jnp.float32), 'Wk': _xavier(ks[4], (D, D)), 'bk': jnp.zeros((D,), jnp.float32), 'Wv': _xavier(ks[5], (D, D)), 'bv': jnp.zeros((D,), jnp.float32), 'Wo': _xavier(ks[6], (D, D)), 'bo': jnp.zeros((D,), jnp.float32)}
    _L1_gnn_all = _L1_gnn_setup()
    _L1_gnn_in = {k: v for k, v in _L1_gnn_all.items() if k in ('Wq', 'bq', 'Wk', 'bk', 'Wv', 'bv', 'Wo', 'bo')}
    del _L1_gnn_all
    return {'x': x, 'src': src, 'dst': dst, 'edge_attr_128': edge_attr_128, 'edge_weight1': edge_weight1, 'L0_gnn_u': _L0_gnn_in['u'], 'L0_gnn_W1': _L0_gnn_in['W1'], 'L0_gnn_b1': _L0_gnn_in['b1'], 'L0_gnn_g1': _L0_gnn_in['g1'], 'L0_gnn_be1': _L0_gnn_in['be1'], 'L0_gnn_W2': _L0_gnn_in['W2'], 'L0_gnn_b2': _L0_gnn_in['b2'], 'L0_gnn_g2': _L0_gnn_in['g2'], 'L0_gnn_be2': _L0_gnn_in['be2'], 'L1_gnn_Wq': _L1_gnn_in['Wq'], 'L1_gnn_bq': _L1_gnn_in['bq'], 'L1_gnn_Wk': _L1_gnn_in['Wk'], 'L1_gnn_bk': _L1_gnn_in['bk'], 'L1_gnn_Wv': _L1_gnn_in['Wv'], 'L1_gnn_bv': _L1_gnn_in['bv'], 'L1_gnn_Wo': _L1_gnn_in['Wo'], 'L1_gnn_bo': _L1_gnn_in['bo']}

def reference(x, src, dst, edge_attr_128, edge_weight1, L0_gnn_u, L0_gnn_W1, L0_gnn_b1, L0_gnn_g1, L0_gnn_be1, L0_gnn_W2, L0_gnn_b2, L0_gnn_g2, L0_gnn_be2, L1_gnn_Wq, L1_gnn_bq, L1_gnn_Wk, L1_gnn_bk, L1_gnn_Wv, L1_gnn_bv, L1_gnn_Wo, L1_gnn_bo):
    import jax
    import jax.numpy as jnp

    def _L0_gnn_ref(x, edge_index, edge_attr, u, batch, W1, b1, g1, be1, W2, b2, g2, be2):
        import jax, jax.numpy as jnp
        import numpy as np
        N_NODES = 50000
        N_EDGES = 10000
        C = 128
        BN_EPS = 0.0001

        def elu(x):
            return jnp.where(x > 0, x, jnp.expm1(x))

        def batchnorm_train(x, gamma, beta):
            mean = jnp.mean(x, axis=0)
            var = jnp.mean((x - mean) ** 2, axis=0)
            return gamma * (x - mean) * jax.lax.rsqrt(var + BN_EPS) + beta
        row, col = (edge_index[0], edge_index[1])
        h = jnp.concatenate([x[row], edge_attr], axis=1)
        h = elu(batchnorm_train(h @ W1 + b1, g1, be1))
        sums = jax.ops.segment_sum(h, col, num_segments=x.shape[0])
        cnt = jax.ops.segment_sum(jnp.ones((h.shape[0],), h.dtype), col, num_segments=x.shape[0])
        agg = sums / jnp.maximum(cnt, 1.0)[:, None]
        z = jnp.concatenate([x, agg], axis=1)
        return elu(batchnorm_train(z @ W2 + b2, g2, be2))

    def _L1_gnn_ref(feats, edge_index, edge_attr, Wq, bq, Wk, bk, Wv, bv, Wo, bo):
        import jax, jax.numpy as jnp
        import numpy as np
        import math
        N = 100000
        E = 25000
        D = 128
        H = 8
        HD = D // H
        EPS = 1e-16

        def _xavier(key, shape):
            fan_out, fan_in = shape
            lim = math.sqrt(6.0 / (fan_in + fan_out))
            return jax.random.uniform(key, shape, jnp.float32, -lim, lim)
        n = feats.shape[0]
        q = (feats @ Wq.T + bq).reshape(n, H, HD)
        k = (feats @ Wk.T + bk).reshape(n, H, HD)
        v = (feats @ Wv.T + bv).reshape(n, H, HD)
        r = edge_index[:, 0]
        c = edge_index[:, 1]
        scores = jnp.einsum('ehd,ehd->eh', q[c], k[r]) / math.sqrt(HD)
        smax = jax.ops.segment_max(scores, c, num_segments=n)
        ex = jnp.exp(scores - smax[c])
        ssum = jax.ops.segment_sum(ex, c, num_segments=n)
        alpha = ex / (ssum[c] + EPS)
        out = jax.ops.segment_sum(alpha[:, :, None] * v[r], c, num_segments=n)
        out = out.reshape(n, D) @ Wo.T + bo
        return out
    edge_index = jnp.stack([src, dst])
    edge_index_t = jnp.stack([src, dst], axis=1)
    batch0 = jnp.zeros((100000,), jnp.int32)
    h = jnp.maximum(_layernorm(x, axis=-1), 0.0)
    x = x + _L0_gnn_ref(h, edge_index, edge_attr_128, L0_gnn_u, batch0, L0_gnn_W1, L0_gnn_b1, L0_gnn_g1, L0_gnn_be1, L0_gnn_W2, L0_gnn_b2, L0_gnn_g2, L0_gnn_be2)
    h = jnp.maximum(_layernorm(x, axis=-1), 0.0)
    x = x + _L1_gnn_ref(h, edge_index_t, edge_weight1, L1_gnn_Wq, L1_gnn_bq, L1_gnn_Wk, L1_gnn_bk, L1_gnn_Wv, L1_gnn_bv, L1_gnn_Wo, L1_gnn_bo)
    return x

_drawn_inputs = setup_inputs


def setup_inputs(seed=0):
    import zlib

    import numpy as np

    out = dict(_drawn_inputs(seed))
    spreads = {'L0_gnn_b1': (0.0, 2.0),
     'L0_gnn_g1': (1.0, 0.2),
     'L0_gnn_be1': (0.0, 0.1),
     'L0_gnn_b2': (0.0, 2.0),
     'L0_gnn_g2': (1.0, 0.2),
     'L0_gnn_be2': (0.0, 0.1),
     'L1_gnn_bq': (0.0, 2.0),
     'L1_gnn_bk': (0.0, 2.0),
     'L1_gnn_bv': (0.0, 0.1),
     'L1_gnn_bo': (0.0, 0.1)}
    factors = {'L1_gnn_Wq': 3.35, 'L1_gnn_Wk': 3.301}
    for name, (base, spread) in spreads.items():
        noise = np.random.default_rng([zlib.crc32(name.encode()), seed]).standard_normal(out[name].shape)
        drawn = base * np.exp(spread * noise) if base else spread * noise
        out[name] = jnp.asarray(drawn.astype(out[name].dtype))
    for name, factor in factors.items():
        out[name] = (out[name] * factor).astype(out[name].dtype)
    return out
```

```python
import concourse.bass as bass
from concourse import mybir
from contextlib import ExitStack

f32 = mybir.dt.float32
i32 = mybir.dt.int32
bf16 = mybir.dt.bfloat16
ALU = mybir.AluOpType
ACT = mybir.ActivationFunctionType
ds = bass.ds

N, E, D, H = 100000, 25000, 128, 8
HD = D // H
LN_EPS, BN_EPS, SM_EPS = 1e-5, 1e-4, 1e-16
T = 16
ROWS = 128 * T
NCH = -(-N // ROWS)
LAST = N - ROWS
DUP = (NCH * ROWS - N) // T
GR = T // 4
TP = 125
TE = 4
CE = TP * TE
ECH = E // CE
NT = E // TP
ROWE = 2 * TP
RE = E // ROWE
PAD = 16
SLOT = 512
BIG = 1.0e30
SKIP = 131072.0


def skewed(eng, chunks, ahead, behind, turn=2):
    def straight(c):
        if c + 1 < chunks:
            ahead(c + 1, (c + 1) % turn)
        behind(c, c % turn)
    turns = (chunks - 2) // turn
    ahead(0, 0)
    for c in range(turn):
        straight(c)
    with eng.Fori(1, turns) as i:
        for k in range(turn):
            ahead(turn * i + (k + 1), (k + 1) % turn)
            behind(turn * i + k, k)
    for c in range(turn * turns, chunks):
        straight(c)


def indexed(pool, chunks, waits, copy_indices, transfers):
    def straight(c):
        waits(c, c % 4)
        if c + 1 < chunks:
            copy_indices(c + 1, (c + 1) % 4)
        transfers(c, c % 4)
    turns = (chunks - 2) // 4
    copy_indices(0, 0)
    for c in range(4):
        straight(c)
    with pool.Fori(1, turns) as i:
        for k in range(4):
            waits(4 * i + k, k)
            copy_indices(4 * i + (k + 1), (k + 1) % 4)
            transfers(4 * i + k, k)
    for c in range(4 * turns, chunks):
        straight(c)


def paired(eng, chunks, step):
    step(0, 0)
    step(1, 1)
    with eng.Fori(1, chunks // 2) as i:
        for k in range(2):
            step(2 * i + k, k)
    if chunks % 2:
        step(chunks - 1, (chunks - 1) % 2)


def filled(c, s, dmas=1):
    return 8 * dmas * (c - s) + 16 * dmas


def wait_emptied(eng, sema, c, s, dmas=1):
    if not isinstance(c, int) or c >= 2:
        eng.wait_ge(sema, 8 * dmas * (c - s))


def wait_before(eng, sema, c):
    if not isinstance(c, int) or c >= 1:
        eng.wait_ge(sema, c)


def program(nc, x, src, dst, edge_attr, W1, b1, g1, be1, W2, b2, g2, be2, Wq, bq, Wk, bk, Wv, bv, Wo, bo, out):
    rows_d = nc.dram_tensor("rows_d", (3, E), f32, kind="Internal").ap()
    xd_d = nc.dram_tensor("xd_d", (E, D), f32, kind="Internal").ap()
    x1_d = nc.dram_tensor("x1_d", (E, D), f32, kind="Internal").ap()
    fin_d = nc.dram_tensor("fin_d", (E, D), f32, kind="Internal").ap()
    CONT, NOTAIL, TC = range(3)

    ctx = ExitStack()
    with ctx:
        def sb(name, shape, dt=f32):
            return ctx.enter_context(nc.sbuf_tensor(name, shape, dt))[tuple(slice(None) for _ in shape)]

        def sem(name):
            return ctx.enter_context(nc.semaphore(name))

        bank = [ctx.enter_context(nc.psum_tensor(f"bank{i}", [128, 512], f32))[:, :] for i in range(8)]

        store = sb("store", [128, PAD + SLOT * ECH + PAD])
        ident = sb("ident", [128, 128])
        ones = sb("ones", [128, 128])
        blk = sb("blk", [128, 128])
        epsc = sb("epsc", [128, 4])
        w1a, w1b, w2a, w2b = (sb(n, [128, 128]) for n in ("w1a", "w1b", "w2a", "w2b"))
        wqT, wkT, wvT, woT = (sb(n, [128, 128]) for n in ("wqT", "wkT", "wvT", "woT"))
        cols = sb("cols", [128, 9])
        B1, G1, BE1, B2, G2, BE2, BQ, BK, BV = range(9)
        bob = sb("bob", [128, 128])
        bom = sb("bom", [128, 128])
        srci = sb("srci", [TP, NT], i32)
        dsti = sb("dsti", [TP, NT], i32)
        scai = sb("scai", [TP, NT], i32)
        tailc = sb("tailc", [TP, NT])
        mean = sb("mean", [128, NCH * T])
        rstd = sb("rstd", [128, NCH * T])
        bns = sb("bns", [128, ECH * 6])
        w2s = sb("w2s", [128, 128])
        shift = sb("shift", [96, 512], bf16)
        ones_b = sb("ones_b", [96, 128], bf16)
        bn = sb("bn", [128, 16])
        S1, T1, T1P, S2, T2, T2P = range(6)

        xa = [sb(f"xa{s}", [128, T, 128]) for s in range(2)]
        hn = [sb(f"hn{s}", [128, T, 130]) for s in range(2)]
        xp = [sb(f"xp{s}", [128, T, 128]) for s in range(2)]
        buf = [sb(f"buf{i}", [128, 512]) for i in range(14)]
        gram = [sb(f"gram{s}", [TP, TE, 258]) for s in range(2)]
        st = [sb(f"st{s}", [128, T, 6]) for s in range(2)]
        ln = [sb(f"ln{s}", [128, 7, T]) for s in range(2)]
        MSUM, MDIF, M2, SQ, VAR, STD, RS = range(7)
        lnm = [sb(f"lnm{s}", [128, T]) for s in range(2)]
        idx = [sb(f"idx{k}", [TP, TE], i32) for k in range(4)]
        zrow = sb("zrow", [1, 512])

        def tiles(b):
            return b[0:TP, 0:TE * 128].rearrange("p (t f) -> p t f", t=TE)

        def moments(dve, s, P, t, n, sums, squares, var, mean_out=None):
            a, w = st[s], ln[s]
            nc.vector.tensor_tensor(w[0:P, MSUM, 0:t], a[0:P, 0:t, 1], a[0:P, 0:t, 4], ALU.add)
            nc.vector.tensor_tensor(w[0:P, MDIF, 0:t], a[0:P, 0:t, 1], a[0:P, 0:t, 4], ALU.subtract)
            nc.vector.tensor_tensor(w[0:P, M2, 0:t], a[0:P, 0:t, 2], a[0:P, 0:t, 5], ALU.add).then_inc(sums, 1)
            dve.wait_ge(sums, n)
            nc.vector.tensor_scalar(lnm[s][0:P, 0:t], w[0:P, MSUM, 0:t], 0.5, None, ALU.mult)
            nc.vector.tensor_tensor(w[0:P, SQ, 0:t], w[0:P, MDIF, 0:t], w[0:P, MDIF, 0:t], ALU.mult).then_inc(squares, 1)
            dve.wait_ge(squares, n)
            nc.vector.scalar_tensor_tensor(w[0:P, VAR, 0:t], w[0:P, SQ, 0:t], 32.0, w[0:P, M2, 0:t],
                                           ALU.mult, ALU.add).then_inc(var, 1)

        def stddev(s, P, t):
            return nc.scalar.activation(ln[s][0:P, STD, 0:t], ln[s][0:P, VAR, 0:t], ACT.Sqrt,
                                        bias=epsc[0:P, 0:1], scale=1.0 / 128)

        load_w, load_c, load_i = sem("load_w"), sem("load_c"), sem("load_i")
        marks_set, zeroed, drawn, p_masks = sem("marks_set"), sem("zeroed"), sem("drawn"), sem("p_masks")
        v_step, t_done, c_done, rows_st = sem("v_step"), sem("t_done"), sem("c_done"), sem("rows_st")
        wraw = [buf[i][:, 0:128] for i in range(4)]
        raw = [xa[0][0:RE, 2 * i:2 * i + 2, :].rearrange("p a b -> p (a b)")[:, 0:ROWE].bitcast(i32) for i in range(4)]
        SRC, DST, PREV, NEXT = range(4)
        fl = [xa[1][0:RE, 2 * i:2 * i + 2, :].rearrange("p a b -> p (a b)")[:, 0:ROWE] for i in range(8)]
        SF, DF, PF, NF, LOC, PM, CNT, SC = range(8)
        mk = [xp[0][0:RE, 2 * i:2 * i + 2, :].rearrange("p a b -> p (a b)")[:, 0:ROWE] for i in range(8)]
        CO, TA, NTA, INV, TCV, ZE, ON, _ = range(8)
        row = xp[1][0:1, 0:4, :].rearrange("p a b -> p (a b)")
        with nc.Block() as block:
            @block.sync
            def _(sp):
                sp.wait_ge(marks_set, 1)
                sp.dma_start(raw[SRC], src.rearrange("(r e) -> r e", e=ROWE)).then_inc(load_i, 16)
                sp.dma_start(raw[DST], dst.rearrange("(r e) -> r e", e=ROWE)).then_inc(load_i, 16)
                sp.dma_start(raw[PREV][1:RE, :], dst[ROWE - 1:E - 1].rearrange("(r e) -> r e", e=ROWE)).then_inc(load_i, 16)
                sp.dma_start(raw[PREV][0:1, 1:ROWE], dst[0:ROWE - 1].rearrange("(o e) -> o e", o=1)).then_inc(load_i, 16)
                sp.dma_start(raw[NEXT][0:RE - 1, :], dst[1:E - ROWE + 1].rearrange("(r e) -> r e", e=ROWE)).then_inc(load_i, 16)
                sp.dma_start(raw[NEXT][RE - 1:RE, 0:ROWE - 1], dst[E - ROWE + 1:E].rearrange("(o e) -> o e", o=1)).then_inc(load_i, 16)
                sp.wait_ge(p_masks, 1)
                for r, m in ((CONT, CO), (NOTAIL, NTA), (TC, TCV)):
                    sp.dma_start(rows_d[r].rearrange("(r e) -> r e", e=ROWE), mk[m]).then_inc(rows_st, 16)
                sp.wait_ge(rows_st, 48)

            @block.scalar
            def _(act):
                for w, a in ((w1a, W1[0:D, :]), (w1b, W1[D:2 * D, :]), (w2a, W2[0:D, :]), (w2b, W2[D:2 * D, :]),
                             (wraw[0], Wq), (wraw[1], Wk), (wraw[2], Wv), (wraw[3], Wo)):
                    act.dma_start(w, a).then_inc(load_w, 16)
                for i, b in enumerate((b1, g1, be1, b2, g2, be2, bq, bk, bv)):
                    act.dma_start(cols[:, i:i + 1], b.rearrange("(p o) -> p o", o=1)).then_inc(load_c, 16)
                act.dma_start(bob[:, :], bo.partition_broadcast(128)).then_inc(load_c, 16)

            @block.gpsimd
            def _(pool):
                nc.gpsimd.memset(ident[:, :], 0.0)
                nc.gpsimd.memset(blk[:, :], HD ** -0.5)
                nc.gpsimd.memset(ones[:, :], 1.0).then_inc(zeroed, 1)
                pool.wait_ge(zeroed, 1)
                nc.gpsimd.affine_select(out=ident[:, :], in_=ident[:, :], compare_op=ALU.not_equal, fill=1.0,
                                        base=0, pattern=[[-1, 128]], channel_multiplier=1).then_inc(drawn, 1)
                bv3 = blk[:, :].rearrange("p (h d) -> p h d", h=H)
                nc.gpsimd.affine_select(out=bv3, in_=bv3, compare_op=ALU.is_ge, fill=0.0,
                                        base=0, pattern=[[-HD, H], [0, HD]], channel_multiplier=1).then_inc(drawn, 1)
                pool.wait_ge(drawn, 2)
                nc.gpsimd.affine_select(out=bv3, in_=bv3, compare_op=ALU.is_ge, fill=0.0,
                                        base=HD - 1, pattern=[[HD, H], [0, HD]], channel_multiplier=-1).then_inc(drawn, 1)
                pool.wait_ge(drawn, 3)

            @block.vector
            def _(dve):
                step = [0]

                def chained(ins):
                    step[0] += 1
                    ins.then_inc(v_step, 1)
                    dve.wait_ge(v_step, step[0])

                nc.vector.memset(raw[PREV], -1)
                nc.vector.memset(raw[NEXT], -1).then_inc(marks_set, 1)
                nc.vector.memset(mk[ZE], 0.0)
                nc.vector.memset(mk[ON], 1.0)
                nc.vector.memset(epsc[:, 0:1], LN_EPS)
                nc.vector.memset(epsc[:, 1:2], BN_EPS)
                nc.vector.memset(epsc[:, 2:3], -1.0)
                nc.vector.memset(epsc[:, 3:4], 0.0)
                nc.vector.memset(zrow[:, :], 0.0)
                nc.vector.memset(ones_b[:, :], 1.0)
                nc.vector.memset(shift[:, :], 0.0)
                nc.vector.memset(row[0:1, 200:201], 0.0)
                nc.vector.memset(store[:, 0:PAD], 0.0)
                nc.vector.memset(store[:, PAD + SLOT * ECH:], 0.0)
                for s in range(2):
                    nc.vector.memset(hn[s][:, :, 128:129], 1.0)
                    nc.vector.memset(gram[s][:, :, 256:257], 1.0)
                dve.wait_ge(load_c, 160)
                nc.vector.tensor_scalar(bom[:, :], bob[:, :], -1.0, None, ALU.add)
                dve.wait_ge(load_i, 96)
                for a, b in ((SF, SRC), (DF, DST), (PF, PREV), (NF, NEXT)):
                    last = nc.vector.tensor_copy(fl[a], raw[b])
                chained(last)
                nc.vector.tensor_tensor(mk[CO], fl[DF], fl[PF], ALU.is_equal)
                chained(nc.vector.tensor_tensor(mk[NTA], fl[DF], fl[NF], ALU.is_equal))
                nc.vector.tensor_scalar(mk[TA], mk[NTA], -1.0, 1.0, ALU.mult, ALU.add)
                nc.vector.tensor_tensor_scan(fl[LOC], mk[CO], mk[ON], 0.0, ALU.mult, ALU.add)
                chained(nc.vector.tensor_tensor_scan(fl[PM], mk[CO], mk[ZE], 1.0, ALU.mult, ALU.add))
                nc.vector.scalar_tensor_tensor(fl[SC], mk[NTA], SKIP, fl[DF], ALU.mult, ALU.add)
                dve.wait_ge(t_done, 1)
                chained(nc.vector.tensor_copy(row[0:1, 0:200], bank[0][0:1, 0:200]))
                nc.vector.tensor_tensor_scan(row[0:1, 201:201 + RE], row[0:1, RE:2 * RE], row[0:1, 0:RE], 0.0,
                                             ALU.mult, ALU.add).then_inc(c_done, 1)
                dve.wait_ge(t_done, 2)
                chained(nc.vector.scalar_tensor_tensor(fl[CNT], fl[PM], bank[1][0:RE, 0:1], fl[LOC], ALU.mult, ALU.add))
                chained(nc.vector.reciprocal(mk[INV], fl[CNT]))
                nc.vector.tensor_tensor(mk[TCV], mk[INV], mk[TA], ALU.mult).then_inc(p_masks, 1)
                for q, o in enumerate((srci, dsti, scai, tailc)):
                    dve.wait_ge(t_done, 3 + q)
                    for j in range(2):
                        nc.vector.tensor_copy(o[:, :].rearrange("p (r j) -> p j r", j=2)[:, j, :],
                                              bank[2 + q][0:TP, j * 128:j * 128 + RE])
                dve.wait_ge(t_done, 7)
                for q, w in enumerate((wqT, wkT, wvT, woT)):
                    last = nc.vector.tensor_copy(w[:, :], bank[6][:, q * 128:(q + 1) * 128])
                chained(last)

            @block.tensor
            def _(pe):
                pe.wait_ge(drawn, 1)
                pe.wait_ge(v_step, 3)
                nc.tensor.matmul(bank[0][0:1, 0:RE], fl[LOC][:, ROWE - 1:ROWE], ident[0:RE, 0:RE], start=True, stop=True)
                nc.tensor.matmul(bank[0][0:1, RE:2 * RE], fl[PM][:, ROWE - 1:ROWE], ident[0:RE, 0:RE],
                                 start=True, stop=True).then_inc(t_done, 1)
                pe.wait_ge(c_done, 1)
                nc.tensor.matmul(bank[1][0:RE, 0:1], row[0:1, 200:200 + RE], ones[0:1, 0:1],
                                 start=True, stop=True).then_inc(t_done, 1)
                pe.wait_ge(v_step, 4)
                for q, m in enumerate((fl[SF], fl[DF], fl[SC], mk[TA])):
                    for j in range(2):
                        last = nc.tensor.transpose(bank[2 + q][0:TP, j * 128:j * 128 + RE], m[:, j * TP:(j + 1) * TP],
                                                   ident[0:RE, 0:RE])
                    last.then_inc(t_done, 1)
                pe.wait_ge(load_w, 128)
                for q in range(4):
                    last = nc.tensor.transpose(bank[6][:, q * 128:(q + 1) * 128], wraw[q], ident[:, :])
                last.then_inc(t_done, 1)

        gram_h = bank[7]
        a_load = [sem(f"a_load{s}") for s in range(2)]
        a_cut, a_sums, a_sq, a_var, a_std, a_rs = (sem("a_" + n) for n in ("cut", "sums", "sq", "var", "std", "rs"))
        a_norm, a_relu, a_gram, a_kept = (sem("a_" + n) for n in ("norm", "relu", "gram", "kept"))

        def base(c):
            return LAST if isinstance(c, int) and c == NCH - 1 else c * ROWS

        with nc.Block() as block:
            @block.sync
            def _(sp):
                def load(c, s):
                    sp.wait_ge(a_norm, c + 1)
                    sp.dma_start(xa[s][:, :, :],
                                 x[ds(base(c), ROWS), :].rearrange("(p j) f -> p j f", j=T)).then_inc(a_load[s], 16)
                paired(sp, NCH, load)

            @block.vector
            def _(dve):
                dve.sem_inc(a_norm, 2)

                def stats(c, s):
                    dve.wait_ge(a_load[s], filled(c, s))
                    for j in range(T):
                        last = nc.vector.bn_stats(st[s][:, j, :], xa[s][:, j, :])
                    last.then_inc(a_cut, 1)
                    dve.wait_ge(a_cut, c + 1)
                    dve.wait_ge(a_kept, c + 1)
                    moments(dve, s, 128, T, c + 1, a_sums, a_sq, a_var)

                def normalize(c, s):
                    dve.wait_ge(a_std, c + 1)
                    nc.vector.reciprocal(ln[s][:, RS, :], ln[s][:, STD, :]).then_inc(a_rs, 1)
                    dve.wait_ge(a_rs, c + 1)
                    dve.wait_ge(a_gram, c + 1)
                    for j in range(T):
                        last = nc.vector.tensor_scalar(hn[s][:, j, 0:128], xa[s][:, j, :], lnm[s][:, j:j + 1],
                                                       ln[s][:, RS, j:j + 1], ALU.subtract, ALU.mult)
                    last.then_inc(a_norm, 1)
                skewed(dve, NCH, stats, normalize)

            @block.gpsimd
            def _(pool):
                pool.sem_inc(a_kept, 2)

                def keep(c, s):
                    pool.wait_ge(a_rs, c + 1)
                    nc.gpsimd.tensor_copy(mean[:, ds(c * T, T)], lnm[s][:, :])
                    nc.gpsimd.tensor_copy(rstd[:, ds(c * T, T)], ln[s][:, RS, :]).then_inc(a_kept, 1)
                paired(pool, NCH, keep)

            @block.scalar
            def _(act):
                def std(c, s):
                    act.wait_ge(a_var, c + 1)
                    stddev(s, 128, T).then_inc(a_std, 1)

                def relu(c, s):
                    act.wait_ge(a_norm, c + 3)
                    nc.scalar.activation(hn[s][:, :, 0:128], hn[s][:, :, 0:128], ACT.Relu).then_inc(a_relu, 1)
                    if isinstance(c, int) and c == NCH - 1:
                        act.wait_ge(a_relu, c + 1)
                        nc.scalar.activation(hn[s][0:DUP, :, 0:129], hn[s][0:DUP, :, 0:129], ACT.Relu,
                                             scale=-1.0).then_inc(a_relu, 1)
                skewed(act, NCH, std, relu)

            @block.tensor
            def _(pe):
                pe.sem_inc(a_gram, 2)
                nc.tensor.matmul(gram_h[:, 0:129], zrow[0:1, 0:128], zrow[0:1, 0:129], start=True, stop=False)

                def products(c, s):
                    last_chunk = isinstance(c, int) and c == NCH - 1
                    pe.wait_ge(a_relu, c + (2 if last_chunk else 1))
                    for j in range(T):
                        last = nc.tensor.matmul(gram_h[:, 0:129], hn[s][:, j, 0:128], hn[s][:, j, 0:129], start=False,
                                                stop=last_chunk and j == T - 1)
                    last.then_inc(a_gram, 1)
                paired(pe, NCH, products)

        b_load = [sem(f"b_load{s}") for s in range(2)]
        b_attr = [sem(f"b_attr{s}") for s in range(2)]
        b_idx, b_cut, b_sums, b_sq, b_var, b_std, b_rs = (sem("b_" + n) for n in ("idx", "cut", "sums", "sq", "var", "std", "rs"))
        b_norm, b_tr, b_ht, b_u, b_put = (sem("b_" + n) for n in ("norm", "tr", "ht", "u", "put"))
        b_bns, b_step, b_col = sem("b_bns"), sem("b_step"), sem("b_col")

        def chunk(c, first=0, n=CE):
            return store[:, ds(c * SLOT + (PAD + first), n)]

        def fetches(pool, index, table, dest, free, idx_sem, load_sems):
            def waits(c, k):
                free(c, k % 2)
                pool.wait_ge(idx_sem, c + 1)

            def copy_indices(c, k):
                nc.gpsimd.tensor_copy(idx[k][:, :], index[:, ds(c * TE, TE)]).then_inc(idx_sem, 1)

            def transfers(c, k):
                for t in range(TE):
                    nc.gpsimd.indirect_dma_start(dest[k % 2][:, t, :], None, table[:, :],
                                                 bass.IndirectOffsetOnAxis(ap=idx[k][:, t:t + 1], axis=0)
                                                 ).then_inc(load_sems[k % 2], 16)
            return waits, copy_indices, transfers

        with nc.Block() as block:
            gx, ea, hT, eT = ([tiles(buf[q + s]) for s in range(2)] for q in (0, 2, 4, 6))
            hT, eT = ([buf[q + s][:, 0:CE] for s in range(2)] for q in (4, 6))
            pT, pA, pU = ([bank[q + s] for s in range(2)] for q in (0, 2, 4))

            @block.sync
            def _(sp):
                def load(c, s):
                    sp.wait_ge(b_tr, c + 1)
                    sp.dma_start(ea[s], edge_attr[ds(c * CE, CE), :].rearrange("(t p) f -> p t f", p=TP)).then_inc(b_attr[s], 16)
                paired(sp, ECH, load)

            @block.gpsimd
            def _(pool):
                def free(c, s):
                    pool.wait_ge(b_tr, c + 1)
                indexed(pool, ECH, *fetches(pool, srci, x, gx, free, b_idx, b_load))

            @block.vector
            def _(dve):
                dve.sem_inc(b_norm, 2)

                def stats(c, s):
                    dve.wait_ge(b_load[s], filled(c, s, TE))
                    for t in range(TE):
                        last = nc.vector.bn_stats(st[s][0:TP, t, :], gx[s][:, t, :])
                    last.then_inc(b_cut, 1)
                    dve.wait_ge(b_cut, c + 1)
                    moments(dve, s, TP, TE, c + 1, b_sums, b_sq, b_var)

                def normalize(c, s):
                    dve.wait_ge(b_std, c + 1)
                    nc.vector.reciprocal(ln[s][0:TP, RS, 0:TE], ln[s][0:TP, STD, 0:TE]).then_inc(b_rs, 1)
                    dve.wait_ge(b_rs, c + 1)
                    for t in range(TE):
                        last = nc.vector.tensor_scalar(gx[s][:, t, :], gx[s][:, t, :], lnm[s][0:TP, t:t + 1],
                                                       ln[s][0:TP, RS, t:t + 1], ALU.subtract, ALU.mult)
                    last.then_inc(b_norm, 1)
                skewed(dve, ECH, stats, normalize)

                def sweep(c, s):
                    dve.wait_ge(b_put, c + 3)
                    nc.vector.bn_stats(bns[:, ds(c * 6, 6)], chunk(c)).then_inc(b_bns, 1)
                paired(dve, ECH, sweep)
                dve.wait_ge(b_bns, ECH)
                nc.vector.bn_aggr(bn[:, 8:10], bns[:, :]).then_inc(b_col, 1)
                dve.wait_ge(b_col, 2)
                nc.vector.reciprocal(bn[:, 11:12], bn[:, 10:11]).then_inc(b_step, 1)
                dve.wait_ge(b_step, 1)
                nc.vector.tensor_tensor(bn[:, S1:S1 + 1], bn[:, 11:12], cols[:, G1:G1 + 1], ALU.mult).then_inc(b_step, 1)
                dve.wait_ge(b_step, 2)
                nc.vector.tensor_tensor(bn[:, 12:13], bn[:, S1:S1 + 1], bn[:, 8:9], ALU.mult).then_inc(b_step, 1)
                dve.wait_ge(b_step, 3)
                nc.vector.tensor_tensor(bn[:, T1:T1 + 1], cols[:, BE1:BE1 + 1], bn[:, 12:13], ALU.subtract).then_inc(b_step, 1)
                dve.wait_ge(b_step, 4)
                nc.vector.tensor_scalar(bn[:, T1P:T1P + 1], bn[:, T1:T1 + 1], 1.0, None, ALU.add)

            @block.scalar
            def _(act):
                act.sem_inc(b_ht, 2)
                act.sem_inc(b_put, 2)

                def std(c, s):
                    act.wait_ge(b_var, c + 1)
                    stddev(s, TP, TE).then_inc(b_std, 1)

                def evacuate(c, s):
                    act.wait_ge(b_tr, c + 3)
                    act.wait_ge(b_u, c + 1)
                    nc.scalar.activation(hT[s], pT[s][:, 0:CE], ACT.Relu)
                    nc.scalar.copy(eT[s], pA[s][:, 0:CE]).then_inc(b_ht, 1)
                    act.wait_ge(b_u, c + 3)
                    nc.scalar.activation(chunk(c), pU[s][:, 0:CE], ACT.Identity, bias=cols[:, B1:B1 + 1]).then_inc(b_put, 1)
                skewed(act, ECH, std, evacuate)
                act.wait_ge(b_col, 1)
                nc.scalar.activation(bn[:, 10:11], bn[:, 9:10], ACT.Sqrt, bias=epsc[:, 1:2]).then_inc(b_col, 1)

            @block.tensor
            def _(pe):
                pe.sem_inc(b_tr, 2)
                pe.sem_inc(b_u, 2)

                def transpose(c, s):
                    pe.wait_ge(b_norm, c + 3)
                    pe.wait_ge(b_attr[s], filled(c, s))
                    pe.wait_ge(b_ht, c + 1)
                    for src_t, to in ((gx[s], pT[s]), (ea[s], pA[s])):
                        for t in range(TE):
                            last = nc.tensor.transpose(to[:, t * TP:(t + 1) * TP], src_t[:, t, :], ident[0:TP, 0:TP])
                    last.then_inc(b_tr, 1)

                def project(c, s):
                    pe.wait_ge(b_ht, c + 3)
                    pe.wait_ge(b_put, c + 1)
                    nc.tensor.matmul(pU[s][:, 0:CE], w1a[:, :], hT[s], start=True, stop=False)
                    nc.tensor.matmul(pU[s][:, 0:CE], w1b[:, :], eT[s], start=False, stop=True).then_inc(b_u, 1)
                skewed(pe, ECH, transpose, project)

        c_cont = [sem(f"c_cont{s}") for s in range(2)]
        c_exp, c_z = sem("c_exp"), sem("c_z")
        c_elu, c_scan = sem("c_elu"), sem("c_scan")

        def row_load(sp, row, c, to, sema):
            sp.dma_start(to, rows_d[row, ds(c * CE, CE)].partition_broadcast(128)).then_inc(sema, 16)

        with nc.Block() as block:
            cb, xe, z = ([buf[q + s][:, 0:CE] for s in range(2)] for q in (0, 2, 4))

            @block.sync
            def _(sp):
                def load(c, s):
                    sp.wait_ge(c_scan, c + 1)
                    row_load(sp, CONT, c, cb[s], c_cont[s])
                paired(sp, ECH, load)

            @block.scalar
            def _(act):
                def exp(c, s):
                    act.wait_ge(c_elu, c + 1)
                    nc.scalar.activation(xe[s], chunk(c), ACT.Exp, scale=bn[:, S1:S1 + 1], bias=bn[:, T1:T1 + 1]).then_inc(c_exp, 1)
                paired(act, ECH, exp)

            @block.vector
            def _(dve):
                dve.sem_inc(c_elu, 2)
                dve.sem_inc(c_scan, 2)

                def affine(c, s):
                    dve.wait_ge(c_scan, c + 1)
                    nc.vector.tensor_scalar(z[s], chunk(c), bn[:, S1:S1 + 1], bn[:, T1P:T1P + 1],
                                            ALU.mult, ALU.add).then_inc(c_z, 1)

                def scan(c, s):
                    dve.wait_ge(c_exp, c + 1)
                    dve.wait_ge(c_z, c + 1)
                    nc.vector.scalar_tensor_tensor(z[s], xe[s], 1.0, z[s], ALU.min, ALU.max).then_inc(c_elu, 1)
                    dve.wait_ge(c_elu, c + 3)
                    dve.wait_ge(c_cont[s], filled(c, s))
                    dve.wait_ge(c_scan, c + 2)
                    nc.vector.tensor_tensor_scan(chunk(c), cb[s], z[s], store[:, ds(c * SLOT + (PAD + CE - SLOT - 1), 1)],
                                                 ALU.mult, ALU.add).then_inc(c_scan, 1)
                skewed(dve, ECH, affine, scan)

        d_rows = [sem(f"d_rows{s}") for s in range(2)]
        d_mul, d_scan, d_put = sem("d_mul"), sem("d_scan"), sem("d_put")

        with nc.Block() as block:
            nb, tb, ts, full = ([buf[q + s][:, 0:CE] for s in range(2)] for q in (0, 2, 4, 6))

            @block.sync
            def _(sp):
                def load(c, s):
                    sp.wait_ge(d_scan, c + 1)
                    row_load(sp, NOTAIL, c * -1 + (ECH - 1), nb[s], d_rows[s])
                    row_load(sp, TC, c * -1 + (ECH - 1), tb[s], d_rows[s])
                paired(sp, ECH, load)

            @block.vector
            def _(dve):
                nc.vector.memset(full[1][:, 0:1], 0.0).then_inc(d_scan, 2)

                def scale(c, s):
                    dve.wait_ge(d_rows[s], filled(c, s, 2))
                    dve.wait_ge(d_scan, c + 1)
                    nc.vector.tensor_tensor(ts[s], chunk(c * -1 + (ECH - 1)), tb[s], ALU.mult).then_inc(d_mul, 1)

                def fill(c, s):
                    dve.wait_ge(d_mul, c + 1)
                    dve.wait_ge(d_scan, c + 2)
                    dve.wait_ge(d_put, c + 1)
                    nc.vector.tensor_tensor_scan(full[s][:, ::-1], nb[s][:, ::-1], ts[s][:, ::-1],
                                                 full[1 - s][:, 0:1], ALU.mult, ALU.add).then_inc(d_scan, 1)
                skewed(dve, ECH, scale, fill)

            @block.scalar
            def _(act):
                act.sem_inc(d_put, 2)

                def put(c, s):
                    act.wait_ge(d_scan, c + 3)
                    nc.scalar.activation(chunk(c * -1 + (ECH - 1)), full[s], ACT.Identity, bias=epsc[:, 2:3]).then_inc(d_put, 1)
                paired(act, ECH, put)

        e_load = [sem(f"e_load{s}") for s in range(2)]
        e_xd = [sem(f"e_xd{s}") for s in range(2)]
        e_idx, e_cut, e_sums, e_sq, e_var, e_std, e_rs = (sem("e_" + n) for n in ("idx", "cut", "sums", "sq", "var", "std", "rs"))
        e_norm, e_at, e_relu, e_tr, e_ht, e_y, e_put, e_agg, e_gram = (
            sem("e_" + n) for n in ("norm", "at", "relu", "tr", "ht", "y", "put", "agg", "gram"))
        gram_e = bank[6]

        with nc.Block() as block:
            gx = [tiles(buf[s]) for s in range(2)]
            hT, aT = ([buf[q + s][:, 0:CE] for s in range(2)] for q in (2, 4))
            pT, pA, pU = ([bank[q + s] for s in range(2)] for q in (0, 2, 4))

            @block.gpsimd
            def _(pool):
                def free(c, s):
                    pool.wait_ge(e_norm, c + 1)
                    wait_emptied(pool, e_xd[s], c, s)
                indexed(pool, ECH, *fetches(pool, dsti, x, gx, free, e_idx, e_load))

            @block.sync
            def _(sp):
                def keep(c, s):
                    sp.wait_ge(e_load[s], filled(c, s, TE))
                    sp.dma_start(xd_d[ds(c * CE, CE), :].rearrange("(t p) f -> p t f", p=TP), gx[s]).then_inc(e_xd[s], 16)
                paired(sp, ECH, keep)
                for s in range(2):
                    sp.wait_ge(e_xd[s], 16 * (ECH // 2))

            @block.vector
            def _(dve):
                dve.sem_inc(e_norm, 2)
                dve.sem_inc(e_agg, 2)

                def stats(c, s):
                    dve.wait_ge(e_load[s], filled(c, s, TE))
                    for t in range(TE):
                        last = nc.vector.bn_stats(st[s][0:TP, t, :], gx[s][:, t, :])
                    last.then_inc(e_cut, 1)
                    dve.wait_ge(e_cut, c + 1)
                    moments(dve, s, TP, TE, c + 1, e_sums, e_sq, e_var)

                def normalize(c, s):
                    dve.wait_ge(e_std, c + 1)
                    nc.vector.reciprocal(ln[s][0:TP, RS, 0:TE], ln[s][0:TP, STD, 0:TE]).then_inc(e_rs, 1)
                    dve.wait_ge(e_rs, c + 1)
                    dve.wait_ge(e_gram, c + 1)
                    for t in range(TE):
                        last = nc.vector.tensor_scalar(gram[s][:, t, 0:128], gx[s][:, t, :], lnm[s][0:TP, t:t + 1],
                                                       ln[s][0:TP, RS, t:t + 1], ALU.subtract, ALU.mult)
                    last.then_inc(e_norm, 1)
                    dve.wait_ge(e_tr, c + 3)
                    nc.vector.tensor_tensor(gram[s][:, :, 128:256], pA[s][0:TP, :].rearrange("p (t f) -> p t f", t=TE),
                                            tailc[:, ds(c * TE, TE)].unsqueeze(2).to_broadcast([TP, TE, 128]),
                                            ALU.mult).then_inc(e_agg, 1)
                skewed(dve, ECH, stats, normalize)

            @block.scalar
            def _(act):
                for q in (e_at, e_relu, e_ht, e_put):
                    act.sem_inc(q, 2)

                def ahead(c, s):
                    act.wait_ge(e_var, c + 1)
                    stddev(s, TP, TE).then_inc(e_std, 1)
                    act.wait_ge(e_y, c + 1)
                    nc.scalar.copy(aT[s], chunk(c)).then_inc(e_at, 1)

                def behind(c, s):
                    act.wait_ge(e_tr, c + 3)
                    nc.scalar.activation(hT[s], pT[s][:, 0:CE], ACT.Relu).then_inc(e_ht, 1)
                    nc.scalar.activation(gram[s][:, :, 0:128], gram[s][:, :, 0:128], ACT.Relu).then_inc(e_relu, 1)
                    act.wait_ge(e_y, c + 3)
                    nc.scalar.copy(store[:, ds(2 * c * (SLOT // 2) + PAD, CE)], pU[s][:, 0:CE]).then_inc(e_put, 1)
                skewed(act, ECH, ahead, behind)

            @block.tensor
            def _(pe):
                for q in (e_tr, e_y, e_gram):
                    pe.sem_inc(q, 2)
                nc.tensor.matmul(gram_e[:, 0:257], zrow[0:1, 0:128], zrow[0:1, 0:257], start=True, stop=False)

                def transpose(c, s):
                    pe.wait_ge(e_norm, c + 3)
                    pe.wait_ge(e_at, c + 3)
                    pe.wait_ge(e_ht, c + 1)
                    pe.wait_ge(e_agg, c + 1)
                    for t in range(TE):
                        nc.tensor.transpose(pT[s][:, t * TP:(t + 1) * TP], gram[s][:, t, 0:128], ident[0:TP, 0:TP])
                    for t in range(TE):
                        last = nc.tensor.transpose(pA[s][0:TP, t * 128:(t + 1) * 128], aT[s][:, t * TP:(t + 1) * TP], ident[:, :])
                    last.then_inc(e_tr, 1)

                def project(c, s):
                    pe.wait_ge(e_ht, c + 3)
                    pe.wait_ge(e_put, c + 1)
                    nc.tensor.matmul(pU[s][:, 0:CE], w2a[:, :], hT[s], start=True, stop=False)
                    nc.tensor.matmul(pU[s][:, 0:CE], w2b[:, :], aT[s], start=False, stop=True).then_inc(e_y, 1)
                    pe.wait_ge(e_agg, c + 3)
                    pe.wait_ge(e_relu, c + 3)
                    for t in range(TE):
                        last = nc.tensor.matmul(gram_e[:, 0:257], gram[s][:, t, 128:256], gram[s][:, t, 0:257], start=False,
                                                stop=isinstance(c, int) and c == ECH - 1 and t == TE - 1)
                    last.then_inc(e_gram, 1)
                skewed(pe, ECH, transpose, project)

        f_v, f_p, f_a, f_b = sem("f_v"), sem("f_p"), sem("f_a"), sem("f_b")
        ghh, gah, gaa, q1, q2, dS, dT, tB, r1, r2, hi_b, mid_b = (
            xa[0][:, i, :] if i < 10 else xa[0][:, i, 0:64].bitcast(bf16) for i in range(12))
        lo_b = xa[0][:, 12, 0:64].bitcast(bf16)
        sums = xa[0][:, 13, :]

        with nc.Block() as block:
            @block.vector
            def _(dve):
                step = [0]

                def chained(ins):
                    step[0] += 1
                    ins.then_inc(f_v, 1)
                    dve.wait_ge(f_v, step[0])

                nc.vector.tensor_copy(ghh, bank[7][:, 0:128])
                nc.vector.tensor_copy(sums[:, 0:1], bank[7][:, 128:129])
                nc.vector.tensor_scalar(gah, bank[6][:, 0:128], 2.0, None, ALU.mult)
                nc.vector.tensor_copy(gaa, bank[6][:, 128:256])
                nc.vector.tensor_copy(sums[:, 1:2], bank[6][:, 256:257]).then_inc(f_b, 1)
                dve.wait_ge(f_p, 1)
                nc.vector.tensor_tensor(q1, bank[0][:, 0:128], w2a[:, :], ALU.mult)
                nc.vector.tensor_tensor(q2, bank[0][:, 128:256], w2b[:, :], ALU.mult).then_inc(f_b, 1)
                dve.wait_ge(f_p, 2)
                chained(nc.vector.tensor_scalar(bn[:, 8:10], bank[1][:, 0:2], 1.0 / N, None, ALU.mult))
                nc.vector.tensor_tensor(bn[:, 13:14], bn[:, 8:9], cols[:, B2:B2 + 1], ALU.add)
                chained(nc.vector.tensor_tensor(bn[:, 12:13], bn[:, 8:9], bn[:, 8:9], ALU.mult))
                nc.vector.tensor_tensor(bn[:, 10:11], bn[:, 9:10], bn[:, 12:13], ALU.subtract).then_inc(f_b, 1)
                dve.wait_ge(f_a, 1)
                chained(nc.vector.reciprocal(bn[:, 11:12], bn[:, 14:15]))
                nc.vector.tensor_tensor(bn[:, 12:13], cols[:, B2:B2 + 1], bn[:, 13:14], ALU.subtract)
                chained(nc.vector.tensor_tensor(bn[:, S2:S2 + 1], bn[:, 11:12], cols[:, G2:G2 + 1], ALU.mult))
                chained(nc.vector.scalar_tensor_tensor(bn[:, T2:T2 + 1], bn[:, 12:13], bn[:, S2:S2 + 1],
                                                       cols[:, BE2:BE2 + 1], ALU.mult, ALU.add))
                chained(nc.vector.tensor_scalar(bn[:, T2P:T2P + 1], bn[:, T2:T2 + 1], 1.0, None, ALU.add))
                nc.vector.tensor_scalar(dS, ident[:, :], bn[:, S2:S2 + 1], None, ALU.mult)
                nc.vector.tensor_scalar(dT, ident[:, :], bn[:, T2P:T2P + 1], None, ALU.mult).then_inc(f_b, 1)
                dve.wait_ge(f_p, 3)
                nc.vector.tensor_tensor(w2s[:, :], w2a[:, :], bank[2][:, 0:128], ALU.mult)
                nc.vector.tensor_copy(tB, bank[2][:, 128:256])
                chained(nc.vector.tensor_copy(hi_b, bank[2][:, 128:256]))
                chained(nc.vector.tensor_tensor(r1, tB, hi_b, ALU.subtract))
                chained(nc.vector.tensor_copy(mid_b, r1))
                chained(nc.vector.tensor_tensor(r2, r1, mid_b, ALU.subtract))
                chained(nc.vector.tensor_copy(lo_b, r2))
                for p, part in ((0, hi_b), (32, mid_b), (64, lo_b)):
                    for g in range(4):
                        last = nc.vector.tensor_copy(shift[p:p + 1, g * 128:(g + 1) * 128], part[p:p + 1, :])
                chained(last)

            @block.scalar
            def _(act):
                act.wait_ge(f_b, 3)
                nc.scalar.activation(bn[:, 14:15], bn[:, 10:11], ACT.Sqrt, bias=epsc[:, 1:2]).then_inc(f_a, 1)

            @block.tensor
            def _(pe):
                pe.wait_ge(f_b, 1)
                nc.tensor.matmul(bank[0][:, 0:128], ghh, w2a[:, :], start=True, stop=False)
                nc.tensor.matmul(bank[0][:, 0:128], gah, w2b[:, :], start=False, stop=True)
                nc.tensor.matmul(bank[0][:, 128:256], gaa, w2b[:, :], start=True, stop=True).then_inc(f_p, 1)
                nc.tensor.matmul(bank[1][:, 0:1], w2a[:, :], sums[:, 0:1], start=True, stop=False)
                nc.tensor.matmul(bank[1][:, 0:1], w2b[:, :], sums[:, 1:2], start=False, stop=True)
                pe.wait_ge(f_b, 2)
                nc.tensor.matmul(bank[1][:, 1:2], q1, ones[:, 0:1], start=True, stop=False)
                nc.tensor.matmul(bank[1][:, 1:2], q2, ones[:, 0:1], start=False, stop=True).then_inc(f_p, 1)
                pe.wait_ge(f_b, 4)
                nc.tensor.matmul(bank[2][:, 0:128], ones[:, :], dS, start=True, stop=True)
                nc.tensor.matmul(bank[2][:, 128:256], ones[:, :], dT, start=True, stop=True).then_inc(f_p, 1)

        g_load = [sem(f"g_load{s}") for s in range(2)]
        g_store = [sem(f"g_store{s}") for s in range(2)]
        g_norm, g_xp, g_tr, g_ht, g_y, g_exp, g_elu, g_sum = (
            sem("g_" + n) for n in ("norm", "xp", "tr", "ht", "y", "exp", "elu", "sum"))

        with nc.Block() as block:
            hT, xe, wv = ([buf[q + s] for s in range(2)] for q in (0, 2, 4))
            pT, pY = ([bank[q + s] for s in range(2)] for q in (0, 2))

            @block.sync
            def _(sp):
                def load(c, s):
                    sp.wait_ge(g_norm, GR * c + GR)
                    sp.wait_ge(g_xp, GR * c + GR)
                    sp.dma_start(xa[s][:, :, :],
                                 x[ds(base(c), ROWS), :].rearrange("(p j) f -> p j f", j=T)).then_inc(g_load[s], 16)

                def keep(c, s):
                    sp.wait_ge(g_sum, GR * c + GR)
                    first = DUP if isinstance(c, int) and c == NCH - 1 else 0
                    sp.dma_start(out[ds(base(c) + first * T, ROWS - first * T), :].rearrange("(p j) f -> p j f", j=T),
                                 xp[s][first:128, :, :]).then_inc(g_store[s], 16)
                skewed(sp, NCH, load, keep)
                for s in range(2):
                    sp.wait_ge(g_store[s], 16 * ((NCH + 1 - s) // 2))

            @block.gpsimd
            def _(pool):
                pool.sem_inc(g_xp, 2 * GR)

                def add_bias(c, s):
                    pool.wait_ge(g_load[s], filled(c, s))
                    wait_emptied(pool, g_store[s], c, s)
                    nc.gpsimd.tensor_tensor(xp[s][:, :, :], xa[s][:, :, :],
                                            bom[:, :].unsqueeze(1).to_broadcast([128, T, 128]), ALU.add).then_inc(g_xp, GR)
                paired(pool, NCH, add_bias)

            @block.vector
            def _(dve):
                dve.sem_inc(g_norm, 2 * GR)
                dve.sem_inc(g_elu, 2)

                def normalize(c, s):
                    dve.wait_ge(g_load[s], filled(c, s))
                    dve.wait_ge(g_tr, GR * c + GR)
                    for j in range(T):
                        last = nc.vector.tensor_scalar(hn[s][:, j, 0:128], xa[s][:, j, :], mean[:, ds(c * T + j, 1)],
                                                       rstd[:, ds(c * T + j, 1)], ALU.subtract, ALU.mult)
                        if j % 4 == 3:
                            last.then_inc(g_norm, 1)

                def combine(c, s):
                    dve.wait_ge(g_xp, GR * c + 3 * GR)
                    for g in range(GR):
                        n, b = GR * c + g, g % 2
                        dve.wait_ge(g_exp, n + 3)
                        nc.vector.scalar_tensor_tensor(wv[b][:, :], xe[b][:, :], 1.0, pY[b][:, :], ALU.min, ALU.max).then_inc(g_elu, 1)
                        dve.wait_ge(g_elu, n + 3)
                        o = xp[s][:, g * 4:(g + 1) * 4, :].rearrange("p t f -> p (t f)")
                        nc.vector.tensor_tensor(o, wv[b][:, :], o, ALU.add).then_inc(g_sum, 1)
                skewed(dve, NCH, normalize, combine)

            @block.scalar
            def _(act):
                for q in (g_ht, g_exp):
                    act.sem_inc(q, 2)

                def relu(n, k):
                    b = k % 2
                    act.wait_ge(g_tr, n + 2 * GR + 1)
                    act.wait_ge(g_y, n + 1)
                    nc.scalar.activation(hT[b][:, :], pT[b][:, :], ACT.Relu).then_inc(g_ht, 1)

                def exp(n, k):
                    b = k % 2
                    act.wait_ge(g_y, n + 3)
                    act.wait_ge(g_elu, n + 1)
                    nc.scalar.activation(xe[b][:, :], pY[b][:, :], ACT.Exp, bias=epsc[:, 2:3]).then_inc(g_exp, 1)
                skewed(act, NCH * GR, relu, exp, turn=2 * GR)

            @block.tensor
            def _(pe):
                pe.sem_inc(g_tr, 2 * GR)
                pe.sem_inc(g_y, 2)

                def transpose(n, k):
                    b, s, g = k % 2, k // GR % 2, k % GR
                    pe.wait_ge(g_norm, n + 2 * GR + 1)
                    pe.wait_ge(g_ht, n + 1)
                    for t in range(4):
                        last = nc.tensor.transpose(pT[b][:, t * 128:(t + 1) * 128], hn[s][:, 4 * g + t, 0:128], ident[:, :])
                    last.then_inc(g_tr, 1)

                def project(n, k):
                    b = k % 2
                    pe.wait_ge(g_elu, n + 1)
                    nc.tensor.matmul(pY[b][:, :], ones_b[:, :], shift[:, :], start=True, stop=False)
                    pe.wait_ge(g_ht, n + 3)
                    for t in range(4):
                        last = nc.tensor.matmul(pY[b][:, t * 128:(t + 1) * 128], hT[b][:, t * 128:(t + 1) * 128], w2s[:, :],
                                                start=False, stop=t == 3)
                    last.then_inc(g_y, 1)
                skewed(pe, NCH * GR, transpose, project, turn=2 * GR)

        h_xd, h_keep, h_scat = ([sem(f"h_{n}{s}") for s in range(2)] for n in ("xd", "keep", "scat"))
        h_exp, h_z, h_elu, h_tr, h_x1, h_o, h_idx = (sem("h_" + n) for n in ("exp", "z", "elu", "tr", "x1", "o", "idx"))

        def puts(pool, rows, ready, idx_sem, scat_sems):
            def waits(c, k):
                ready(c, k % 2)
                pool.wait_ge(idx_sem, c + 1)

            def copy_indices(c, k):
                nc.gpsimd.tensor_copy(idx[k][:, :], scai[:, ds(c * TE, TE)]).then_inc(idx_sem, 1)

            def transfers(c, k):
                for t in range(TE):
                    nc.gpsimd.indirect_dma_start(out[:, :], bass.IndirectOffsetOnAxis(ap=idx[k][:, t:t + 1], axis=0),
                                                 rows[k % 2][:, t, :], None, bounds_check=N - 1, oob_is_err=False
                                                 ).then_inc(scat_sems[k % 2], 16)
            return waits, copy_indices, transfers

        with nc.Block() as block:
            xe, z = ([buf[q + s][:, 0:CE] for s in range(2)] for q in (0, 2))
            xd, x1, ob = ([tiles(buf[q + s]) for s in range(2)] for q in (4, 6, 8))
            pX = [bank[s] for s in range(2)]

            @block.sync
            def _(sp):
                def load(c, s):
                    sp.wait_ge(h_x1, c + 1)
                    sp.dma_start(xd[s], xd_d[ds(c * CE, CE), :].rearrange("(t p) f -> p t f", p=TP)).then_inc(h_xd[s], 16)

                def keep(c, s):
                    sp.wait_ge(h_x1, c + 3)
                    sp.dma_start(x1_d[ds(c * CE, CE), :].rearrange("(t p) f -> p t f", p=TP), x1[s]).then_inc(h_keep[s], 16)
                skewed(sp, ECH, load, keep)
                for s in range(2):
                    sp.wait_ge(h_keep[s], 16 * (ECH // 2))

            @block.scalar
            def _(act):
                def exp(c, s):
                    act.wait_ge(h_elu, c + 1)
                    nc.scalar.activation(xe[s], chunk(c), ACT.Exp, scale=bn[:, S2:S2 + 1], bias=bn[:, T2:T2 + 1]).then_inc(h_exp, 1)
                paired(act, ECH, exp)

            @block.tensor
            def _(pe):
                pe.sem_inc(h_tr, 2)

                def transpose(c, s):
                    pe.wait_ge(h_elu, c + 3)
                    pe.wait_ge(h_x1, c + 1)
                    for t in range(TE):
                        last = nc.tensor.transpose(pX[s][0:TP, t * 128:(t + 1) * 128], z[s][:, t * TP:(t + 1) * TP], ident[:, :])
                    last.then_inc(h_tr, 1)
                paired(pe, ECH, transpose)

            @block.vector
            def _(dve):
                dve.sem_inc(h_elu, 2)
                dve.sem_inc(h_x1, 2)

                def elu(c, s):
                    dve.wait_ge(h_tr, c + 1)
                    nc.vector.tensor_scalar(z[s], chunk(c), bn[:, S2:S2 + 1], bn[:, T2P:T2P + 1],
                                            ALU.mult, ALU.add).then_inc(h_z, 1)
                    dve.wait_ge(h_z, c + 1)
                    dve.wait_ge(h_exp, c + 1)
                    nc.vector.scalar_tensor_tensor(z[s], xe[s], 1.0, z[s], ALU.min, ALU.max).then_inc(h_elu, 1)

                def add(c, s):
                    dve.wait_ge(h_tr, c + 3)
                    dve.wait_ge(h_xd[s], filled(c, s))
                    wait_emptied(dve, h_keep[s], c, s)
                    nc.vector.tensor_tensor(x1[s], pX[s][0:TP, :].rearrange("p (t f) -> p t f", t=TE), xd[s], ALU.add).then_inc(h_x1, 1)
                    dve.wait_ge(h_x1, c + 3)
                    wait_emptied(dve, h_scat[s], c, s, TE)
                    nc.vector.tensor_tensor(ob[s], x1[s], bom[0:TP, :].unsqueeze(1).to_broadcast([TP, TE, 128]),
                                            ALU.add).then_inc(h_o, 1)
                skewed(dve, ECH, elu, add)

            @block.gpsimd
            def _(pool):
                def ready(c, s):
                    pool.wait_ge(h_o, c + 1)
                indexed(pool, ECH, *puts(pool, ob, ready, h_idx, h_scat))
                for s in range(2):
                    pool.wait_ge(h_scat[s], 16 * TE * (ECH // 2))

        i_load, i_x1, i_cont, i_fin = ([sem(f"i_{n}{s}") for s in range(2)] for n in ("load", "x1", "cont", "fin"))
        i_idx, i_sub, i_cut, i_sums, i_sq, i_var, i_std, i_rs = (
            sem("i_" + n) for n in ("idx", "sub", "cut", "sums", "sq", "var", "std", "rs"))
        i_norm, i_tr, i_ht, i_q, i_qs, i_kv, i_kq, i_s, i_nb, i_max, i_diff, i_exp, i_w, i_sum, i_rec, i_attn, i_o, i_xb, i_out = (
            sem("i_" + n) for n in ("norm", "tr", "ht", "q", "qs", "kv", "kq", "s", "nb", "max", "diff", "exp", "w", "sum",
                                    "rec", "attn", "o", "xb", "out"))

        def quarter(b, k):
            return b[:, 4 * k:4 * (k + 1), :].rearrange("p t f -> p (t f)")

        with nc.Block() as block:
            gx, x1, hd = ([tiles(buf[q + s]) for s in range(2)] for q in (0, 2, 4))
            hs, ht, cb = ([buf[q + s][:, 0:CE] for s in range(2)] for q in (6, 8, 10))
            fin = [tiles(buf[12 + s]) for s in range(2)]
            mx = [xa[s][:, 0:4, :].rearrange("p t f -> p (t f)")[:, 0:CE + 1] for s in range(2)]
            oo = [quarter(xa[s], 1)[:, 0:CE] for s in range(2)]
            ll = [quarter(xa[s], 2)[:, 0:CE] for s in range(2)]
            xb = [tiles(quarter(xa[s], 3)) for s in range(2)]
            nb, qs, kq, dd = (quarter(xp[0], k)[:, 0:CE] for k in range(4))
            ee, wv, rr, aa = (quarter(xp[1], k)[:, 0:CE] for k in range(4))
            pHs, pHt, pQ, pK, pV, pS, pO = (bank[k] for k in range(7))

            @block.sync
            def _(sp):
                def load(c, s):
                    sp.wait_ge(i_out, c + 1)
                    sp.dma_start(x1[s], x1_d[ds(c * CE, CE), :].rearrange("(t p) f -> p t f", p=TP)).then_inc(i_x1[s], 16)
                    row_load(sp, CONT, c, cb[s], i_cont[s])

                def keep(c, s):
                    sp.wait_ge(i_out, c + 3)
                    sp.dma_start(fin_d[ds(c * CE, CE), :].rearrange("(t p) f -> p t f", p=TP), fin[s]).then_inc(i_fin[s], 16)
                skewed(sp, ECH, load, keep)
                for s in range(2):
                    sp.wait_ge(i_fin[s], 16 * (ECH // 2))

            @block.gpsimd
            def _(pool):
                def free(c, s):
                    pool.wait_ge(i_tr, c + 1)
                waits, copy_indices, transfers = fetches(pool, srci, out, gx, free, i_idx, i_load)

                def transfers_and_bias(c, k):
                    transfers(c, k)
                    pool.wait_ge(i_x1[k % 2], filled(c, k % 2))
                    pool.wait_ge(i_out, c + 1)
                    nc.gpsimd.tensor_tensor(xb[k % 2], x1[k % 2], bom[0:TP, :].unsqueeze(1).to_broadcast([TP, TE, 128]),
                                            ALU.add).then_inc(i_xb, 1)
                indexed(pool, ECH, waits, copy_indices, transfers_and_bias)

            @block.vector
            def _(dve):
                dve.sem_inc(i_norm, 2)
                dve.sem_inc(i_out, 2)
                for s in range(2):
                    nc.vector.memset(mx[s], 0.0)
                    nc.vector.memset(ll[s], 0.0)
                    last = nc.vector.memset(oo[s], 0.0)
                last.then_inc(i_nb, 1)
                dve.wait_ge(i_nb, 1)

                def stats(c, s):
                    dve.wait_ge(i_load[s], filled(c, s, TE))
                    nc.vector.tensor_tensor(gx[s], gx[s], bob[0:TP, :].unsqueeze(1).to_broadcast([TP, TE, 128]),
                                            ALU.subtract).then_inc(i_sub, 1)
                    dve.wait_ge(i_x1[s], filled(c, s))
                    for t in range(TE):
                        nc.vector.bn_stats(st[s][0:TP, TE + t, :], x1[s][:, t, :])
                    dve.wait_ge(i_sub, c + 1)
                    for t in range(TE):
                        last = nc.vector.bn_stats(st[s][0:TP, t, :], gx[s][:, t, :])
                    last.then_inc(i_cut, 1)
                    dve.wait_ge(i_cut, c + 1)
                    moments(dve, s, TP, 2 * TE, c + 1, i_sums, i_sq, i_var)
                    dve.wait_ge(i_std, c + 1)
                    nc.vector.reciprocal(ln[s][0:TP, RS, 0:2 * TE], ln[s][0:TP, STD, 0:2 * TE]).then_inc(i_rs, 1)
                    dve.wait_ge(i_rs, c + 1)
                    dve.wait_ge(i_tr, c + 1)
                    for t in range(TE):
                        nc.vector.tensor_scalar(gx[s][:, t, :], gx[s][:, t, :], lnm[s][0:TP, t:t + 1],
                                                ln[s][0:TP, RS, t:t + 1], ALU.subtract, ALU.mult)
                        last = nc.vector.tensor_scalar(hd[s][:, t, :], x1[s][:, t, :], lnm[s][0:TP, TE + t:TE + t + 1],
                                                       ln[s][0:TP, RS, TE + t:TE + t + 1], ALU.subtract, ALU.mult)
                    last.then_inc(i_norm, 1)

                def attend(c, s):
                    dve.wait_ge(i_cont[s], filled(c, s))
                    nc.vector.tensor_scalar(nb, cb[s], BIG, -BIG, ALU.mult, ALU.add)
                    nc.vector.tensor_copy(mx[s][:, 0:1], mx[1 - s][:, CE:CE + 1]).then_inc(i_nb, 1)
                    dve.wait_ge(i_kv, c + 1)
                    dve.wait_ge(i_qs, c + 1)
                    nc.vector.scalar_tensor_tensor(kq, pK[:, 0:CE], cols[:, BK:BK + 1], qs, ALU.add, ALU.mult).then_inc(i_kq, 1)
                    dve.wait_ge(i_s, c + 1)
                    dve.wait_ge(i_nb, c + 2)
                    nc.vector.tensor_tensor_scan(mx[s][:, 1:CE + 1], nb, pS[:, 0:CE], mx[1 - s][:, CE:CE + 1],
                                                 ALU.add, ALU.max).then_inc(i_max, 1)
                    dve.wait_ge(i_max, c + 1)
                    nc.vector.tensor_tensor(ee, pS[:, 0:CE], mx[s][:, 1:CE + 1], ALU.subtract)
                    nc.vector.tensor_tensor(dd, mx[s][:, 0:CE], mx[s][:, 1:CE + 1], ALU.subtract).then_inc(i_diff, 1)
                    dve.wait_ge(i_exp, c + 1)
                    nc.vector.scalar_tensor_tensor(dd, dd, 1.0, cb[s], ALU.min, ALU.mult)
                    nc.vector.scalar_tensor_tensor(wv, pV[:, 0:CE], cols[:, BV:BV + 1], ee, ALU.add, ALU.mult).then_inc(i_w, 1)
                    dve.wait_ge(i_w, c + 1)
                    nc.vector.tensor_tensor_scan(ll[s], dd, ee, ll[1 - s][:, CE - 1:CE], ALU.mult, ALU.add)
                    nc.vector.tensor_tensor_scan(oo[s], dd, wv, oo[1 - s][:, CE - 1:CE], ALU.mult, ALU.add).then_inc(i_sum, 1)
                    dve.wait_ge(i_sum, c + 1)
                    nc.vector.tensor_scalar(rr, ll[s], SM_EPS, None, ALU.add).then_inc(i_rec, 1)
                    dve.wait_ge(i_rec, 2 * c + 1)
                    nc.vector.reciprocal(rr, rr).then_inc(i_rec, 1)
                    dve.wait_ge(i_rec, 2 * c + 2)
                    nc.vector.tensor_tensor(aa, oo[s], rr, ALU.mult).then_inc(i_attn, 1)
                    dve.wait_ge(i_o, c + 1)
                    dve.wait_ge(i_xb, c + 1)
                    wait_emptied(dve, i_fin[s], c, s)
                    nc.vector.tensor_tensor(fin[s], pO[0:TP, :].rearrange("p (t f) -> p t f", t=TE), xb[s], ALU.add).then_inc(i_out, 1)
                skewed(dve, ECH, stats, attend)

            @block.scalar
            def _(act):
                def std(c, s):
                    act.wait_ge(i_var, c + 1)
                    stddev(s, TP, 2 * TE).then_inc(i_std, 1)

                def behind(c, s):
                    act.wait_ge(i_tr, c + 3)
                    nc.scalar.activation(hs[s], pHs[:, 0:CE], ACT.Relu)
                    nc.scalar.activation(ht[s], pHt[:, 0:CE], ACT.Relu).then_inc(i_ht, 1)
                    act.wait_ge(i_q, c + 1)
                    nc.scalar.activation(qs, pQ[:, 0:CE], ACT.Identity, bias=cols[:, BQ:BQ + 1]).then_inc(i_qs, 1)
                    act.wait_ge(i_diff, c + 1)
                    nc.scalar.activation(ee, ee, ACT.Exp)
                    nc.scalar.activation(dd, dd, ACT.Exp).then_inc(i_exp, 1)
                skewed(act, ECH, std, behind)

            @block.tensor
            def _(pe):
                pe.sem_inc(i_tr, 2)

                def transpose(c, s):
                    pe.wait_ge(i_norm, c + 3)
                    wait_before(pe, i_ht, c)
                    for src_t, to in ((gx[s], pHs), (hd[s], pHt)):
                        for t in range(TE):
                            last = nc.tensor.transpose(to[:, t * TP:(t + 1) * TP], src_t[:, t, :], ident[0:TP, 0:TP])
                    last.then_inc(i_tr, 1)

                def project(c, s):
                    pe.wait_ge(i_ht, c + 1)
                    nc.tensor.matmul(pQ[:, 0:CE], wqT[:, :], ht[s], start=True, stop=True).then_inc(i_q, 1)
                    wait_before(pe, i_w, c)
                    nc.tensor.matmul(pK[:, 0:CE], wkT[:, :], hs[s], start=True, stop=True)
                    nc.tensor.matmul(pV[:, 0:CE], wvT[:, :], hs[s], start=True, stop=True).then_inc(i_kv, 1)
                    pe.wait_ge(i_kq, c + 1)
                    nc.tensor.matmul(pS[:, 0:CE], blk[:, :], kq, start=True, stop=True).then_inc(i_s, 1)
                    pe.wait_ge(i_attn, c + 1)
                    for t in range(TE):
                        last = nc.tensor.matmul(pO[0:TP, t * 128:(t + 1) * 128], aa[:, t * TP:(t + 1) * TP], woT[:, :],
                                                start=True, stop=True)
                    last.then_inc(i_o, 1)
                skewed(pe, ECH, transpose, project)

        j_load, j_scat = ([sem(f"j_{n}{s}") for s in range(2)] for n in ("load", "scat"))
        j_idx = sem("j_idx")

        with nc.Block() as block:
            rows = [tiles(buf[s]) for s in range(2)]

            @block.sync
            def _(sp):
                def load(c, s):
                    wait_emptied(sp, j_scat[s], c, s, TE)
                    sp.dma_start(rows[s], fin_d[ds(c * CE, CE), :].rearrange("(t p) f -> p t f", p=TP)).then_inc(j_load[s], 16)
                paired(sp, ECH, load)

            @block.gpsimd
            def _(pool):
                def ready(c, s):
                    pool.wait_ge(j_load[s], filled(c, s))
                indexed(pool, ECH, *puts(pool, rows, ready, j_idx, j_scat))
                for s in range(2):
                    pool.wait_ge(j_scat[s], 16 * TE * (ECH // 2))


_INS = ["x", "src", "dst", "edge_attr_128", "L0_gnn_W1", "L0_gnn_b1", "L0_gnn_g1", "L0_gnn_be1", "L0_gnn_W2", "L0_gnn_b2",
        "L0_gnn_g2", "L0_gnn_be2", "L1_gnn_Wq", "L1_gnn_bq", "L1_gnn_Wk", "L1_gnn_bk", "L1_gnn_Wv", "L1_gnn_bv", "L1_gnn_Wo",
        "L1_gnn_bo"]


def kernel(**inputs):
    import numpy as np
    import concourse.bacc as bacc
    from concourse.bass_utils import run_bass_kernel_spmd

    nc = bacc.Bacc("TRN2", target_bir_lowering=False, num_devices=1)
    arrays, args = {}, []
    for name in _INS:
        a = np.ascontiguousarray(inputs[name])
        arrays[f"in_{name}"] = a
        args.append(nc.dram_tensor(f"in_{name}", a.shape, mybir.dt.from_np(a.dtype), kind="ExternalInput").ap())
    out = nc.dram_tensor("out_rows", (N, D), f32, kind="ExternalOutput").ap()
    program(nc, *args, out)
    r = run_bass_kernel_spmd(nc, [arrays], core_ids=[0])
    return r.results[0]["out_rows"]
```

```python
import concourse.bass as bass
from concourse import mybir
from contextlib import ExitStack

f32 = mybir.dt.float32
i32 = mybir.dt.int32
bf16 = mybir.dt.bfloat16
ALU = mybir.AluOpType
ACT = mybir.ActivationFunctionType
ds = bass.ds

N, E, D, H = 100000, 25000, 128, 8
HD = D // H
LN_EPS, BN_EPS, SM_EPS = 1e-5, 1e-4, 1e-16
T = 16
ROWS = 128 * T
NCH = -(-N // ROWS)
LAST = N - ROWS
DUP = (NCH * ROWS - N) // T
GR = T // 4
TP = 125
TE = 4
CE = TP * TE
ECH = E // CE
NT = E // TP
ROWE = 2 * TP
RE = E // ROWE
PAD = 16
SLOT = 512
BIG = 1.0e30
SKIP = 131072.0


def pipelined(eng, chunks, stages, turn=4):
    stages = [(stage[0], stage[1], stage[2] if len(stage) > 2 else chunks) for stage in stages]
    lag = max(l for l, _, _ in stages)

    def straight(n):
        for l, step, own in stages:
            if 0 <= n - l < own:
                step(n - l, (n - l) % turn)
    first, last, back = -(-(lag + turn) // turn), (chunks - 1) // turn, -(-lag // turn)
    for n in range(first * turn):
        straight(n)
    with eng.Fori(first - back, last - back) as i:
        for k in range(turn):
            for l, step, _ in stages:
                step(turn * i + (turn * back + k - l), (k - l) % turn)
    for n in range(last * turn, max(own for _, _, own in stages) + lag):
        straight(n)


def nth(c, back=0):
    return c + (5 - back)


def loaded(c, k, dmas=1):
    return 4 * dmas * (c - k) + 16 * dmas


def wait_stored(eng, sema, c, k, dmas=1):
    if not isinstance(c, int) or c >= 4:
        eng.wait_ge(sema, 4 * dmas * (c - k))


def indexed(pool, chunks, waits, copy_indices, transfers, first=True, rest=True):
    def straight(c):
        waits(c, c % 4)
        if c + 1 < chunks:
            copy_indices(c + 1, (c + 1) % 4)
        transfers(c, c % 4)
    turns = (chunks - 2) // 4
    if first:
        copy_indices(0, 0)
        for c in range(3):
            straight(c)
    if rest:
        straight(3)
        with pool.Fori(1, turns) as i:
            for k in range(4):
                waits(4 * i + k, k)
                copy_indices(4 * i + (k + 1), (k + 1) % 4)
                transfers(4 * i + k, k)
        for c in range(4 * turns, chunks):
            straight(c)


def program(nc, x, src, dst, edge_attr, W1, b1, g1, be1, W2, b2, g2, be2, Wq, bq, Wk, bk, Wv, bv, Wo, bo, out):
    rows_d = nc.dram_tensor("rows_d", (3, E), f32, kind="Internal").ap()
    cont_d = nc.dram_tensor("cont_d", (E,), bf16, kind="Internal").ap()
    xd_d = nc.dram_tensor("xd_d", (E, D), f32, kind="Internal").ap()
    x1_d = nc.dram_tensor("x1_d", (E, D), f32, kind="Internal").ap()
    s_d = nc.dram_tensor("s_d", (ECH, 128, CE), f32, kind="Internal").ap()
    m_d = nc.dram_tensor("m_d", (ECH, 128, CE + 1), f32, kind="Internal").ap()
    q_d = nc.dram_tensor("q_d", (ECH, 128, CE), f32, kind="Internal").ap()
    CONT, NOTAIL, TC = range(3)

    ctx = ExitStack()
    with ctx:
        def sb(name, shape, dt=f32):
            return ctx.enter_context(nc.sbuf_tensor(name, shape, dt))[tuple(slice(None) for _ in shape)]

        held = []

        def sem(name):
            held.append(nc.alloc_semaphore(name=name))
            return held[-1]

        def release(count):
            nc.clear_and_free_semaphores(held[:count])
            del held[:count]

        bank = [ctx.enter_context(nc.psum_tensor(f"bank{i}", [128, 512], f32))[:, :] for i in range(8)]

        store = sb("store", [128, PAD + SLOT * ECH + PAD])
        ident = sb("ident", [128, 128])
        ones = sb("ones", [128, 128])
        blk = sb("blk", [128, 128])
        epsc = sb("epsc", [128, 4])
        w1a, w1b, w2a, w2b = (sb(n, [128, 128]) for n in ("w1a", "w1b", "w2a", "w2b"))
        wqT, wkT, wvT, woT = (sb(n, [128, 128]) for n in ("wqT", "wkT", "wvT", "woT"))
        cols = sb("cols", [128, 9])
        B1, G1, BE1, B2, G2, BE2, BQ, BK, BV = range(9)
        bob = sb("bob", [128, 128])
        bom = sb("bom", [128, 128])
        srci = sb("srci", [TP, NT], i32)
        dsti = sb("dsti", [TP, NT], i32)
        scai = sb("scai", [TP, NT], i32)
        tailc = sb("tailc", [TP, NT])
        nmr = sb("nmr", [128, NCH * T])
        rstd = sb("rstd", [128, NCH * T])
        bns = sb("bns", [128, ECH * 6])
        w2s = sb("w2s", [128, 128])
        shift = sb("shift", [96, 512], bf16)
        ones_b = sb("ones_b", [96, 128], bf16)
        bn = sb("bn", [128, 16])
        S1, T1, T1P, S2, T2, T2P = range(6)

        xa = [sb(f"xa{s}", [128, T, 128]) for s in range(2)]
        hn = [sb(f"hn{s}", [128, T, 130]) for s in range(2)]
        xp = [sb(f"xp{s}", [128, T, 128]) for s in range(2)]
        buf = [sb(f"buf{i}", [128, 512]) for i in range(14)]
        gram = [sb(f"gram{s}", [TP, TE, 258]) for s in range(2)]
        st = [sb(f"st{s}", [128, T + TE if s < 2 else TE, 6]) for s in range(4)]
        ln = [sb(f"ln{s}", [128, 7, T + TE if s < 2 else TE]) for s in range(4)]
        MSUM, MDIF, M2, SQ, VAR, STD, RS = range(7)
        lnm = [sb(f"lnm{s}", [128, T + TE if s < 2 else TE]) for s in range(4)]
        idx = [sb(f"idx{k}", [TP, TE], i32) for k in range(4)]
        zrow = sb("zrow", [1, 260])

        def tiles(b):
            return b[0:TP, 0:TE * 128].rearrange("p (t f) -> p t f", t=TE)

        def moments(dve, P, t, slot, wait_stats, sums, squares, var):
            def add_halves(c, k):
                a, w = st[slot(k)], ln[slot(k)]
                wait_stats(c)
                nc.vector.tensor_tensor(w[0:P, MSUM, 0:t], a[0:P, 0:t, 1], a[0:P, 0:t, 4], ALU.add)
                nc.vector.tensor_tensor(w[0:P, MDIF, 0:t], a[0:P, 0:t, 1], a[0:P, 0:t, 4], ALU.subtract)
                nc.vector.tensor_tensor(w[0:P, M2, 0:t], a[0:P, 0:t, 2], a[0:P, 0:t, 5], ALU.add).then_inc(sums, 1)

            def square(c, k):
                w = ln[slot(k)]
                dve.wait_ge(sums, c + 1)
                nc.vector.tensor_scalar(lnm[slot(k)][0:P, 0:t], w[0:P, MSUM, 0:t], 0.5, None, ALU.mult)
                nc.vector.tensor_tensor(w[0:P, SQ, 0:t], w[0:P, MDIF, 0:t], w[0:P, MDIF, 0:t], ALU.mult).then_inc(squares, 1)

            def variance(c, k):
                w = ln[slot(k)]
                dve.wait_ge(squares, c + 1)
                nc.vector.scalar_tensor_tensor(w[0:P, VAR, 0:t], w[0:P, SQ, 0:t], 32.0, w[0:P, M2, 0:t],
                                               ALU.mult, ALU.add).then_inc(var, 1)
            return add_halves, square, variance

        def stddev(s, P, t):
            return nc.scalar.activation(ln[s][0:P, STD, 0:t], ln[s][0:P, VAR, 0:t], ACT.Sqrt,
                                        bias=epsc[0:P, 0:1], scale=1.0 / 128)

        load_w, load_c, load_i = sem("load_w"), sem("load_c"), sem("load_i")
        marks_set, zeroed, drawn, p_masks = sem("marks_set"), sem("zeroed"), sem("drawn"), sem("p_masks")
        v_step, t_done, c_done, rows_st = sem("v_step"), sem("t_done"), sem("c_done"), sem("rows_st")
        wraw = [buf[i][:, 0:128] for i in range(4)]
        layout = [store[0:RE, PAD + 256 * i:PAD + 256 * i + ROWE] for i in range(20)]
        raw = [a.bitcast(i32) for a in layout[0:4]]
        SRC, DST, PREV, NEXT = range(4)
        fl = layout[4:12]
        SF, DF, PF, NF, LOC, PM, CNT, SC = range(8)
        mk = layout[12:19]
        cont_b = layout[19][:, 0:ROWE // 2].bitcast(bf16)
        CO, TA, NTA, INV, TCV, ZE, ON = range(7)
        row = store[0:1, PAD + 256 * 20:PAD + 256 * 20 + 512]
        xin = [xa[0], xa[1], xp[0], xp[1]]
        a_load = [sem(f"a_load{k}") for k in range(4)]

        def base(c):
            return LAST if isinstance(c, int) and c == NCH - 1 else c * ROWS

        def load_nodes(sp, c, k):
            sp.dma_start(xin[k][:, :, :], x[ds(base(c), ROWS), :].rearrange("(p j) f -> p j f", j=T)).then_inc(a_load[k], 16)

        with nc.Block() as block:
            @block.sync
            def _(sp):
                sp.wait_ge(marks_set, 1)
                sp.dma_start(raw[SRC], src.rearrange("(r e) -> r e", e=ROWE)).then_inc(load_i, 16)
                sp.dma_start(raw[DST], dst.rearrange("(r e) -> r e", e=ROWE)).then_inc(load_i, 16)
                sp.dma_start(raw[PREV][1:RE, :], dst[ROWE - 1:E - 1].rearrange("(r e) -> r e", e=ROWE)).then_inc(load_i, 16)
                sp.dma_start(raw[PREV][0:1, 1:ROWE], dst[0:ROWE - 1].rearrange("(o e) -> o e", o=1)).then_inc(load_i, 16)
                sp.dma_start(raw[NEXT][0:RE - 1, :], dst[1:E - ROWE + 1].rearrange("(r e) -> r e", e=ROWE)).then_inc(load_i, 16)
                sp.dma_start(raw[NEXT][RE - 1:RE, 0:ROWE - 1], dst[E - ROWE + 1:E].rearrange("(o e) -> o e", o=1)).then_inc(load_i, 16)
                sp.wait_ge(load_i, 96)
                for c in range(2):
                    load_nodes(sp, c, c)
                sp.wait_ge(p_masks, 1)
                for r, m in ((CONT, CO), (NOTAIL, NTA), (TC, TCV)):
                    sp.dma_start(rows_d[r].rearrange("(r e) -> r e", e=ROWE), mk[m]).then_inc(rows_st, 16)
                sp.dma_start(cont_d.rearrange("(r e) -> r e", e=ROWE), cont_b).then_inc(rows_st, 16)
                for c in range(2, 4):
                    load_nodes(sp, c, c)
                sp.wait_ge(rows_st, 64)

            @block.scalar
            def _(act):
                for w, a in ((w1a, W1[0:D, :]), (w1b, W1[D:2 * D, :]), (w2a, W2[0:D, :]), (w2b, W2[D:2 * D, :]),
                             (wraw[0], Wq), (wraw[1], Wk), (wraw[2], Wv), (wraw[3], Wo)):
                    act.dma_start(w, a).then_inc(load_w, 16)
                for i, b in enumerate((b1, g1, be1, b2, g2, be2, bq, bk, bv)):
                    act.dma_start(cols[:, i:i + 1], b.rearrange("(p o) -> p o", o=1)).then_inc(load_c, 16)
                act.dma_start(bob[:, :], bo.partition_broadcast(128)).then_inc(load_c, 16)

            @block.gpsimd
            def _(pool):
                nc.gpsimd.memset(ident[:, :], 0.0)
                nc.gpsimd.memset(blk[:, :], HD ** -0.5)
                nc.gpsimd.memset(ones[:, :], 1.0).then_inc(zeroed, 1)
                pool.wait_ge(zeroed, 1)
                nc.gpsimd.affine_select(out=ident[:, :], in_=ident[:, :], compare_op=ALU.not_equal, fill=1.0,
                                        base=0, pattern=[[-1, 128]], channel_multiplier=1).then_inc(drawn, 1)
                bv3 = blk[:, :].rearrange("p (h d) -> p h d", h=H)
                nc.gpsimd.affine_select(out=bv3, in_=bv3, compare_op=ALU.is_ge, fill=0.0,
                                        base=0, pattern=[[-HD, H], [0, HD]], channel_multiplier=1).then_inc(drawn, 1)
                pool.wait_ge(drawn, 2)
                nc.gpsimd.affine_select(out=bv3, in_=bv3, compare_op=ALU.is_ge, fill=0.0,
                                        base=HD - 1, pattern=[[HD, H], [0, HD]], channel_multiplier=-1).then_inc(drawn, 1)
                pool.wait_ge(drawn, 3)

            @block.vector
            def _(dve):
                step = [0]

                def chained(ins):
                    step[0] += 1
                    ins.then_inc(v_step, 1)
                    dve.wait_ge(v_step, step[0])

                nc.vector.memset(raw[PREV], -1)
                nc.vector.memset(raw[NEXT], -1).then_inc(marks_set, 1)
                nc.vector.memset(mk[ZE], 0.0)
                nc.vector.memset(mk[ON], 1.0)
                nc.vector.memset(epsc[:, 0:1], LN_EPS)
                nc.vector.memset(epsc[:, 1:2], BN_EPS)
                nc.vector.memset(epsc[:, 2:3], -1.0)
                nc.vector.memset(epsc[:, 3:4], -BIG)
                nc.vector.memset(zrow[:, :], 0.0)
                nc.vector.memset(ones_b[:, :], 1.0)
                nc.vector.memset(shift[:, :], 0.0)
                nc.vector.memset(row[0:1, 200:201], 0.0)
                nc.vector.memset(store[:, 0:PAD], 0.0)
                nc.vector.memset(store[:, PAD + SLOT * ECH:], 0.0)
                for s in range(2):
                    nc.vector.memset(st[s][:, T:T + TE, :], 0.0)
                    nc.vector.memset(hn[s][:, :, 128:129], 1.0)
                    nc.vector.memset(gram[s][:, :, 256:257], 1.0)
                dve.wait_ge(load_c, 160)
                nc.vector.tensor_scalar(bom[:, :], bob[:, :], -1.0, None, ALU.add)
                dve.wait_ge(load_i, 96)
                for a, b in ((SF, SRC), (DF, DST), (PF, PREV), (NF, NEXT)):
                    last = nc.vector.tensor_copy(fl[a], raw[b])
                chained(last)
                nc.vector.tensor_tensor(mk[CO], fl[DF], fl[PF], ALU.is_equal)
                chained(nc.vector.tensor_tensor(mk[NTA], fl[DF], fl[NF], ALU.is_equal))
                nc.vector.tensor_copy(cont_b, mk[CO])
                nc.vector.tensor_scalar(mk[TA], mk[NTA], -1.0, 1.0, ALU.mult, ALU.add)
                nc.vector.tensor_tensor_scan(fl[LOC], mk[CO], mk[ON], 0.0, ALU.mult, ALU.add)
                chained(nc.vector.tensor_tensor_scan(fl[PM], mk[CO], mk[ZE], 1.0, ALU.mult, ALU.add))
                nc.vector.scalar_tensor_tensor(fl[SC], mk[NTA], SKIP, fl[DF], ALU.mult, ALU.add)
                dve.wait_ge(t_done, 1)
                chained(nc.vector.tensor_copy(row[0:1, 0:200], bank[0][0:1, 0:200]))
                nc.vector.tensor_tensor_scan(row[0:1, 201:201 + RE], row[0:1, RE:2 * RE], row[0:1, 0:RE], 0.0,
                                             ALU.mult, ALU.add).then_inc(c_done, 1)
                dve.wait_ge(t_done, 2)
                chained(nc.vector.scalar_tensor_tensor(fl[CNT], fl[PM], bank[1][0:RE, 0:1], fl[LOC], ALU.mult, ALU.add))
                chained(nc.vector.reciprocal(mk[INV], fl[CNT]))
                nc.vector.tensor_tensor(mk[TCV], mk[INV], mk[TA], ALU.mult).then_inc(p_masks, 1)
                for q, o in enumerate((srci, dsti, scai, tailc)):
                    dve.wait_ge(t_done, 3 + q)
                    for j in range(2):
                        nc.vector.tensor_copy(o[:, :].rearrange("p (r j) -> p j r", j=2)[:, j, :],
                                              bank[2 + q][0:TP, j * 128:j * 128 + RE])
                dve.wait_ge(t_done, 7)
                for q, w in enumerate((wqT, wkT, wvT, woT)):
                    last = nc.vector.tensor_copy(w[:, :], bank[6][:, q * 128:(q + 1) * 128])
                chained(last)

            @block.tensor
            def _(pe):
                pe.wait_ge(drawn, 1)
                pe.wait_ge(v_step, 3)
                nc.tensor.matmul(bank[0][0:1, 0:RE], fl[LOC][:, ROWE - 1:ROWE], ident[0:RE, 0:RE], start=True, stop=True)
                nc.tensor.matmul(bank[0][0:1, RE:2 * RE], fl[PM][:, ROWE - 1:ROWE], ident[0:RE, 0:RE],
                                 start=True, stop=True).then_inc(t_done, 1)
                pe.wait_ge(c_done, 1)
                nc.tensor.matmul(bank[1][0:RE, 0:1], row[0:1, 200:200 + RE], ones[0:1, 0:1],
                                 start=True, stop=True).then_inc(t_done, 1)
                pe.wait_ge(v_step, 4)
                for q, m in enumerate((fl[SF], fl[DF], fl[SC], mk[TA])):
                    for j in range(2):
                        last = nc.tensor.transpose(bank[2 + q][0:TP, j * 128:j * 128 + RE], m[:, j * TP:(j + 1) * TP],
                                                   ident[0:RE, 0:RE])
                    last.then_inc(t_done, 1)
                pe.wait_ge(load_w, 128)
                for q in range(4):
                    last = nc.tensor.transpose(bank[6][:, q * 128:(q + 1) * 128], wraw[q], ident[:, :])
                last.then_inc(t_done, 1)

        gram_h = bank[7]
        AT = 13
        of_preparation = len(held) - len(a_load)
        a_cut, a_sums, a_sq, a_var, a_std, a_rs, a_nm = (sem("a_" + n) for n in ("cut", "sums", "sq", "var", "std", "rs", "nm"))
        a_norm, a_relu, a_gram = (sem("a_" + n) for n in ("norm", "relu", "gram"))

        b_load, b_attr = ([sem(f"b_{n}{k}") for k in range(4)] for n in ("load", "attr"))
        b_idx, b_cut, b_rs = (sem("b_" + n) for n in ("idx", "cut", "rs"))
        b_norm, b_tr, b_ht, b_u, b_put = (sem("b_" + n) for n in ("norm", "tr", "ht", "u", "put"))
        b_bns, b_step, b_col = sem("b_bns"), sem("b_step"), sem("b_col")

        def quarter(b, k):
            w = b.shape[1] * b.shape[2] // 4
            return b[:, :, :].rearrange("p t f -> p (t f)")[:, k * w:(k + 1) * w]

        spare = [quarter(b, k) for b in (xa[0], xa[1], xp[0], xp[1], hn[0], hn[1]) for k in range(4)]

        def in_slot(k):
            return (ECH + 3 - k) // 4

        def edge_rows(a, c):
            return a[ds(c * CE, CE), :].rearrange("(t p) f -> p t f", p=TP)

        def chunk(c, first=0, n=CE):
            return store[:, ds(c * SLOT + (PAD + first), n)]

        def fetches(pool, index, table, dest, free, idx_sem, load_sems, place=lambda c: c):
            def waits(c, k):
                free(c, k)
                pool.wait_ge(idx_sem, c + 1)

            def copy_indices(c, k):
                wait_stored(pool, load_sems[k], c, k, TE)
                nc.gpsimd.tensor_copy(idx[k][:, :], index[:, ds(place(c) * TE, TE)]).then_inc(idx_sem, 1)

            def transfers(c, k):
                for t in range(TE):
                    nc.gpsimd.indirect_dma_start(dest[k][:, t, :], None, table[:, :],
                                                 bass.IndirectOffsetOnAxis(ap=idx[k][:, t:t + 1], axis=0)
                                                 ).then_inc(load_sems[k], 16)
            return waits, copy_indices, transfers

        with nc.Block() as block:
            gx, ea = ([tiles(b) for b in buf[q:q + 4]] for q in (0, 4))
            hT, eT = ([b[:, 0:CE] for b in buf[q:q + 2]] for q in (8, 10))
            pT, pA, pU = (bank[q:q + 2] for q in (0, 2, 4))

            @block.sync
            def _(sp):
                def load(c, k):
                    if isinstance(c, int) and c < 4:
                        return
                    sp.wait_ge(a_norm, nth(c, 4))
                    sp.wait_ge(a_relu, nth(c, 4))
                    load_nodes(sp, c, k)

                def load_attributes(c, k):
                    sp.wait_ge(b_tr, nth(c, 4))
                    sp.dma_start(ea[k], edge_rows(edge_attr, c)).then_inc(b_attr[k], 16)
                pipelined(sp, NCH, [(0, load), (0, load_attributes, ECH)])

            @block.vector
            def _(dve):
                dve.sem_inc(a_norm, 4)
                dve.sem_inc(b_norm, 4)
                dve.sem_inc(b_cut, 4)

                def stats(c, k):
                    s = k % 2
                    dve.wait_ge(a_load[k], loaded(c, k))
                    for j in range(T):
                        last = nc.vector.bn_stats(st[s][:, j, :], xin[k][:, j, :])
                    last.then_inc(a_cut, 1)

                def invert(c, k):
                    dve.wait_ge(a_std, c + 1)
                    nc.vector.reciprocal(rstd[:, ds(c * T, T)], ln[k % 2][:, STD, 0:T]).then_inc(a_rs, 1)

                def negate(c, k):
                    dve.wait_ge(a_rs, c + 1)
                    nc.vector.scalar_tensor_tensor(nmr[:, ds(c * T, T)], lnm[k % 2][:, 0:T], -1.0, rstd[:, ds(c * T, T)],
                                                   ALU.mult, ALU.mult).then_inc(a_nm, 1)

                def normalize(c, k):
                    s = k % 2
                    dve.wait_ge(a_gram, nth(c, 2))
                    dve.wait_ge(a_nm, c + 1)
                    for j in range(AT, T):
                        last = nc.vector.tensor_scalar(hn[s][:, j, 0:128], xin[k][:, j, :], rstd[:, ds(c * T + j, 1)],
                                                       nmr[:, ds(c * T + j, 1)], ALU.mult, ALU.add)
                    last.then_inc(a_norm, 1)

                def edge_stats(c, k):
                    s = k % 2
                    dve.wait_ge(b_load[k], loaded(c, k, TE))
                    for t in range(TE):
                        last = nc.vector.bn_stats(st[s][0:TP, T + t, :], gx[k][:, t, :])
                    last.then_inc(b_cut, 1)

                def edge_invert(c, k):
                    s = k % 2
                    dve.wait_ge(a_std, c + 3)
                    nc.vector.reciprocal(ln[s][0:TP, RS, T:T + TE], ln[s][0:TP, STD, T:T + TE]).then_inc(b_rs, 1)

                def edge_normalize(c, k):
                    s = k % 2
                    dve.wait_ge(b_rs, c + 1)
                    for t in range(TE):
                        last = nc.vector.tensor_scalar(gx[k][:, t, :], gx[k][:, t, :], lnm[s][0:TP, T + t:T + t + 1],
                                                       ln[s][0:TP, RS, T + t:T + t + 1], ALU.subtract, ALU.mult)
                    last.then_inc(b_norm, 1)

                def sweep(c, k):
                    dve.wait_ge(b_put, nth(c))
                    nc.vector.bn_stats(bns[:, ds(c * 6, 6)], chunk(c)).then_inc(b_bns, 1)

                def both(c):
                    dve.wait_ge(a_cut, min(c + 1, NCH) if isinstance(c, int) else c + 1)
                    dve.wait_ge(b_cut, nth(c, 2))
                add_halves, square, variance = moments(dve, 128, T + TE, lambda k: k % 2, both, a_sums, a_sq, a_var)
                pipelined(dve, NCH, [
                    (0, stats), (2, edge_stats, ECH), (1, invert), (3, edge_invert, ECH), (0, add_halves, ECH + 2),
                    (1, negate), (0, square, ECH + 2), (3, edge_normalize, ECH), (0, variance, ECH + 2),
                    (1, normalize), (6, sweep, ECH)])
                dve.wait_ge(b_bns, ECH)
                nc.vector.bn_aggr(bn[:, 8:10], bns[:, :]).then_inc(b_col, 1)
                dve.wait_ge(b_col, 2)
                nc.vector.reciprocal(bn[:, 11:12], bn[:, 10:11]).then_inc(b_step, 1)
                dve.wait_ge(b_step, 1)
                nc.vector.tensor_tensor(bn[:, S1:S1 + 1], bn[:, 11:12], cols[:, G1:G1 + 1], ALU.mult).then_inc(b_step, 1)
                dve.wait_ge(b_step, 2)
                nc.vector.tensor_tensor(bn[:, 12:13], bn[:, S1:S1 + 1], bn[:, 8:9], ALU.mult).then_inc(b_step, 1)
                dve.wait_ge(b_step, 3)
                nc.vector.tensor_tensor(bn[:, T1:T1 + 1], cols[:, BE1:BE1 + 1], bn[:, 12:13], ALU.subtract).then_inc(b_step, 1)
                dve.wait_ge(b_step, 4)
                nc.vector.tensor_scalar(bn[:, T1P:T1P + 1], bn[:, T1:T1 + 1], 1.0, None, ALU.add)


            @block.gpsimd
            def _(pool):
                release(of_preparation)

                def free(c, k):
                    pool.wait_ge(b_tr, nth(c, 4))
                indexed(pool, ECH, *fetches(pool, srci, x, gx, free, b_idx, b_load))

            @block.scalar
            def _(act):
                for q in (a_relu, b_ht, b_put):
                    act.sem_inc(q, 4)

                def std(c, k):
                    act.wait_ge(a_var, c + 1)
                    stddev(k % 2, 128, T + TE).then_inc(a_std, 1)

                def relu(c, k):
                    s = k % 2
                    act.wait_ge(a_nm, c + 1)
                    act.wait_ge(a_gram, nth(c, 2))
                    for j in range(AT):
                        nc.scalar.activation(hn[s][:, j, 0:128], xin[k][:, j, :], ACT.Relu,
                                             scale=rstd[:, ds(c * T + j, 1)], bias=nmr[:, ds(c * T + j, 1)])
                    act.wait_ge(a_norm, nth(c))
                    nc.scalar.activation(hn[s][:, AT:T, 0:128], hn[s][:, AT:T, 0:128], ACT.Relu).then_inc(a_relu, 1)
                    if isinstance(c, int) and c == NCH - 1:
                        act.wait_ge(a_relu, nth(c))
                        nc.scalar.activation(hn[s][0:DUP, :, 0:129], hn[s][0:DUP, :, 0:129], ACT.Relu,
                                             scale=-1.0).then_inc(a_relu, 1)

                def evacuate(c, k):
                    s = k % 2
                    act.wait_ge(b_tr, nth(c))
                    act.wait_ge(b_u, nth(c, 2))
                    nc.scalar.activation(hT[s], pT[s][:, 0:CE], ACT.Relu)
                    nc.scalar.copy(eT[s], pA[s][:, 0:CE]).then_inc(b_ht, 1)

                def put(c, k):
                    act.wait_ge(b_u, nth(c))
                    nc.scalar.activation(chunk(c), pU[k % 2][:, 0:CE], ACT.Identity, bias=cols[:, B1:B1 + 1]).then_inc(b_put, 1)
                pipelined(act, NCH, [(1, relu), (0, std, ECH + 2), (4, evacuate, ECH), (5, put, ECH)])
                act.wait_ge(b_col, 1)
                nc.scalar.activation(bn[:, 10:11], bn[:, 9:10], ACT.Sqrt, bias=epsc[:, 1:2]).then_inc(b_col, 1)


            @block.tensor
            def _(pe):
                for q in (a_gram, b_tr, b_u):
                    pe.sem_inc(q, 4)
                nc.tensor.matmul(gram_h[:, 0:129], zrow[0:1, 0:128], zrow[0:1, 0:129], start=True, stop=False)

                def products(c, k):
                    s, last_chunk = k % 2, isinstance(c, int) and c == NCH - 1
                    pe.wait_ge(a_relu, nth(c, -1 if last_chunk else 0))
                    for j in range(T):
                        last = nc.tensor.matmul(gram_h[:, 0:129], hn[s][:, j, 0:128], hn[s][:, j, 0:129], start=False,
                                                stop=last_chunk and j == T - 1)
                    last.then_inc(a_gram, 1)

                def transpose(c, k):
                    s = k % 2
                    pe.wait_ge(b_norm, nth(c))
                    pe.wait_ge(b_attr[k], loaded(c, k))
                    pe.wait_ge(b_ht, nth(c, 2))
                    for src_t, to in ((gx[k], pT[s]), (ea[k], pA[s])):
                        for t in range(TE):
                            last = nc.tensor.transpose(to[:, t * TP:(t + 1) * TP], src_t[:, t, :], ident[0:TP, 0:TP])
                    last.then_inc(b_tr, 1)

                def project(c, k):
                    s = k % 2
                    pe.wait_ge(b_ht, nth(c))
                    pe.wait_ge(b_put, nth(c, 2))
                    nc.tensor.matmul(pU[s][:, 0:CE], w1a[:, :], hT[s], start=True, stop=False)
                    nc.tensor.matmul(pU[s][:, 0:CE], w1b[:, :], eT[s], start=False, stop=True).then_inc(b_u, 1)
                pipelined(pe, NCH, [(3, transpose, ECH), (1, products), (4, project, ECH)])

        c_cont = [sem(f"c_cont{k}") for k in range(4)]
        c_exp, c_z, c_elu, c_scan = (sem("c_" + n) for n in ("exp", "z", "elu", "scan"))

        def row_load(sp, row, c, to, sema):
            sp.dma_start(to, rows_d[row, ds(c * CE, CE)].partition_broadcast(128)).then_inc(sema, 16)

        e_rows, e_load, e_xd = ([sem(f"e_{n}{k}") for k in range(4)] for n in ("rows", "load", "xd"))
        e_idx, e_cut, e_sums, e_sq, e_var, e_std, e_rs = (sem("e_" + n) for n in ("idx", "cut", "sums", "sq", "var", "std", "rs"))
        e_mul, e_scan, e_norm, e_at, e_relu, e_tr, e_ht, e_y, e_put, e_agg, e_gram = (
            sem("e_" + n) for n in ("mul", "scan", "norm", "at", "relu", "tr", "ht", "y", "put", "agg", "gram"))
        gram_e = bank[6]

        def there(c):
            return c * -1 + (ECH - 1)

        gx, nb, tb = ([v(b) for b in q] for v, q in ((tiles, spare[16:20]), (lambda b: b[:, 0:CE], spare[8:12]),
                                                     (lambda b: b[:, 0:CE], spare[12:16])))
        hT, aT, ts, full = ([b[:, 0:CE] for b in buf[q:q + n]] for q, n in ((0, 2), (2, 4), (6, 2), (8, 2)))
        pair = gram + [b[0:TP, 0:9, :].rearrange("p t f -> p (t f)")[:, 0:TE * 258].rearrange("p (t f) -> p t f", t=TE)
                       for b in xa]
        pT, pA, pU = (bank[q:q + 2] for q in (0, 2, 4))

        def target_rows(pool):
            def free(c, k):
                if not isinstance(c, int) or c >= 4:
                    pool.wait_ge(e_norm, nth(c, 4))
                    wait_stored(pool, e_xd[k], c, k)
            return fetches(pool, dsti, x, gx, free, e_idx, e_load, there)

        def load_spread(sp, c, k):
            row_load(sp, NOTAIL, there(c), nb[k], e_rows[k])
            row_load(sp, TC, there(c), tb[k], e_rows[k])

        with nc.Block() as block:
            cb, xe, z = ([b[:, 0:CE] for b in buf[q:q + 4]] for q in (0, 4, 8))

            @block.sync
            def _(sp):
                def load(c, k):
                    sp.wait_ge(c_scan, nth(c, 4))
                    row_load(sp, CONT, c, cb[k], c_cont[k])
                pipelined(sp, ECH, [(0, load)])
                for c in range(4):
                    load_spread(sp, c, c)

            @block.gpsimd
            def _(pool):
                indexed(pool, ECH, *target_rows(pool), rest=False)

            @block.scalar
            def _(act):
                act.sem_inc(c_exp, 4)

                def exp(c, k):
                    act.wait_ge(c_scan, nth(c, 4))
                    last = nc.scalar.activation(xe[k], chunk(c), ACT.Exp, scale=bn[:, S1:S1 + 1], bias=bn[:, T1:T1 + 1])
                    if k < 3:
                        last = nc.scalar.activation(z[k], chunk(c), ACT.Identity, scale=bn[:, S1:S1 + 1], bias=bn[:, T1P:T1P + 1])
                    last.then_inc(c_exp, 1)
                pipelined(act, ECH, [(0, exp)])

            @block.vector
            def _(dve):
                for q in (c_z, c_elu, c_scan):
                    dve.sem_inc(q, 4)

                def affine(c, k):
                    if k == 3:
                        dve.wait_ge(c_scan, nth(c, 4))
                        nc.vector.tensor_scalar(z[k], chunk(c), bn[:, S1:S1 + 1], bn[:, T1P:T1P + 1],
                                                ALU.mult, ALU.add).then_inc(c_z, 4)

                def elu(c, k):
                    dve.wait_ge(c_exp, nth(c))
                    if k == 3:
                        dve.wait_ge(c_z, nth(c))
                    nc.vector.scalar_tensor_tensor(z[k], xe[k], 1.0, z[k], ALU.min, ALU.max).then_inc(c_elu, 1)

                def scan(c, k):
                    dve.wait_ge(c_elu, nth(c))
                    dve.wait_ge(c_cont[k], loaded(c, k))
                    dve.wait_ge(c_scan, nth(c, 1))
                    nc.vector.tensor_tensor_scan(chunk(c), cb[k], z[k], store[:, ds(c * SLOT + (PAD + CE - SLOT - 1), 1)],
                                                 ALU.mult, ALU.add).then_inc(c_scan, 1)
                pipelined(dve, ECH, [(0, affine), (1, elu), (2, scan)])

        with nc.Block() as block:
            @block.gpsimd
            def _(pool):
                indexed(pool, ECH, *target_rows(pool), first=False)

            @block.sync
            def _(sp):
                def load(c, k):
                    if isinstance(c, int) and c < 4:
                        return
                    sp.wait_ge(e_scan, nth(c, 4))
                    load_spread(sp, c, k)

                def keep(c, k):
                    sp.wait_ge(e_load[k], loaded(c, k, TE))
                    sp.dma_start(edge_rows(xd_d, there(c)), gx[k]).then_inc(e_xd[k], 16)
                pipelined(sp, ECH, [(0, load), (1, keep)])
                for k in range(4):
                    sp.wait_ge(e_xd[k], 16 * in_slot(k))

            @block.vector
            def _(dve):
                for q in (e_mul, e_norm, e_agg):
                    dve.sem_inc(q, 4)
                for b in pair[2:4]:
                    nc.vector.memset(b[:, :, 256:257], 1.0)
                nc.vector.memset(full[1][:, 0:1], 0.0).then_inc(e_scan, 4)

                def scale(c, k):
                    s = k % 2
                    dve.wait_ge(e_rows[k], loaded(c, k, 2))
                    dve.wait_ge(e_scan, nth(c, 2))
                    nc.vector.tensor_tensor(ts[s], chunk(there(c)), tb[k], ALU.mult).then_inc(e_mul, 1)

                def stats(c, k):
                    s = k % 2
                    dve.wait_ge(e_load[k], loaded(c, k, TE))
                    for t in range(TE):
                        last = nc.vector.bn_stats(st[s][0:TP, t, :], gx[k][:, t, :])
                    last.then_inc(e_cut, 1)

                def spread(c, k):
                    s = k % 2
                    dve.wait_ge(e_mul, nth(c))
                    dve.wait_ge(e_scan, nth(c, 1))
                    dve.wait_ge(e_at, nth(c, 2))
                    nc.vector.tensor_tensor_scan(full[s][:, ::-1], nb[k][:, ::-1], ts[s][:, ::-1],
                                                 full[1 - s][:, 0:1], ALU.mult, ALU.add).then_inc(e_scan, 1)

                def invert(c, k):
                    s = k % 2
                    dve.wait_ge(e_std, c + 1)
                    nc.vector.reciprocal(ln[s][0:TP, RS, 0:TE], ln[s][0:TP, STD, 0:TE]).then_inc(e_rs, 1)

                def normalize(c, k):
                    s = k % 2
                    dve.wait_ge(e_rs, c + 1)
                    dve.wait_ge(e_gram, nth(c, 4))
                    for t in range(TE):
                        last = nc.vector.tensor_scalar(pair[k][:, t, 0:128], gx[k][:, t, :], lnm[s][0:TP, t:t + 1],
                                                       ln[s][0:TP, RS, t:t + 1], ALU.subtract, ALU.mult)
                    last.then_inc(e_norm, 1)

                def keep_last(c, k):
                    dve.wait_ge(e_tr, nth(c))
                    nc.vector.tensor_tensor(pair[k][:, :, 128:256], pA[k % 2][0:TP, :].rearrange("p (t f) -> p t f", t=TE),
                                            tailc[:, ds(there(c) * TE, TE)].unsqueeze(2).to_broadcast([TP, TE, 128]),
                                            ALU.mult).then_inc(e_agg, 1)
                add_halves, square, variance = moments(dve, TP, TE, lambda k: k % 2, lambda c: dve.wait_ge(e_cut, c + 1),
                                                       e_sums, e_sq, e_var)
                pipelined(dve, ECH, [(0, scale), (0, stats), (1, invert), (0, spread), (0, add_halves), (1, normalize),
                                     (0, square), (3, keep_last), (0, variance)])

            @block.scalar
            def _(act):
                for q in (e_at, e_relu, e_ht, e_put):
                    act.sem_inc(q, 4)

                def shifted(c, k):
                    act.wait_ge(e_scan, nth(c))
                    act.wait_ge(e_y, nth(c, 4))
                    nc.scalar.activation(aT[k], full[k % 2], ACT.Identity, bias=epsc[:, 2:3]).then_inc(e_at, 1)

                def std(c, k):
                    act.wait_ge(e_var, c + 1)
                    stddev(k % 2, TP, TE).then_inc(e_std, 1)

                def relu(c, k):
                    s = k % 2
                    act.wait_ge(e_tr, nth(c))
                    act.wait_ge(e_y, nth(c, 2))
                    nc.scalar.activation(hT[s], pT[s][:, 0:CE], ACT.Relu).then_inc(e_ht, 1)
                    nc.scalar.activation(pair[k][:, :, 0:128], pair[k][:, :, 0:128], ACT.Relu).then_inc(e_relu, 1)

                def put(c, k):
                    act.wait_ge(e_y, nth(c))
                    nc.scalar.copy(chunk(there(c)), pU[k % 2][:, 0:CE]).then_inc(e_put, 1)
                pipelined(act, ECH, [(0, shifted), (2, relu), (3, put), (0, std)])

            @block.tensor
            def _(pe):
                for q in (e_tr, e_y, e_gram):
                    pe.sem_inc(q, 4)
                nc.tensor.matmul(gram_e[:, 0:257], zrow[0:1, 0:128], zrow[0:1, 0:257], start=True, stop=False)

                def transpose(c, k):
                    s = k % 2
                    pe.wait_ge(e_norm, nth(c))
                    pe.wait_ge(e_at, nth(c))
                    pe.wait_ge(e_ht, nth(c, 2))
                    pe.wait_ge(e_agg, nth(c, 2))
                    for t in range(TE):
                        nc.tensor.transpose(pT[s][:, t * TP:(t + 1) * TP], pair[k][:, t, 0:128], ident[0:TP, 0:TP])
                    for t in range(TE):
                        last = nc.tensor.transpose(pA[s][0:TP, t * 128:(t + 1) * 128], aT[k][:, t * TP:(t + 1) * TP], ident[:, :])
                    last.then_inc(e_tr, 1)

                def project(c, k):
                    s = k % 2
                    pe.wait_ge(e_ht, nth(c))
                    pe.wait_ge(e_put, nth(c, 2))
                    nc.tensor.matmul(pU[s][:, 0:CE], w2a[:, :], hT[s], start=True, stop=False)
                    nc.tensor.matmul(pU[s][:, 0:CE], w2b[:, :], aT[k], start=False, stop=True).then_inc(e_y, 1)

                def products(c, k):
                    pe.wait_ge(e_agg, nth(c))
                    pe.wait_ge(e_relu, nth(c))
                    for t in range(TE):
                        last = nc.tensor.matmul(gram_e[:, 0:257], pair[k][:, t, 128:256], pair[k][:, t, 0:257], start=False,
                                                stop=isinstance(c, int) and c == ECH - 1 and t == TE - 1)
                    last.then_inc(e_gram, 1)
                pipelined(pe, ECH, [(2, transpose), (3, project), (4, products)])

        f_v, f_p, f_a, f_b = sem("f_v"), sem("f_p"), sem("f_a"), sem("f_b")
        scratch = [buf[i // 4][:, i % 4 * 128:i % 4 * 128 + 128] for i in range(14)]
        ghh, gah, gaa, q1, q2, dS, dT, tB, r1, r2 = scratch[0:10]
        hi_b, mid_b, lo_b = (a[:, 0:64].bitcast(bf16) for a in scratch[10:13])
        sums = scratch[13]

        g_load = [sem(f"g_load{k}") for k in range(4)]

        def half(b, k, first=0):
            return b[k // 2][first:128, 8 * (k % 2):8 * (k % 2) + 8, :]

        def nodes(a, m, k, first=0):
            start = LAST if isinstance(m, int) and m >= 2 * NCH - 2 else (m - k % 2) * (ROWS // 2)
            rows = a[ds(start + first * T, ROWS - first * T), :].rearrange("(p j) f -> p j f", j=T)
            return rows[:, 8 * (k % 2):8 * (k % 2) + 8, :]

        def load_half(sp, m, k):
            sp.dma_start(half(xa, k), nodes(x, m, k)).then_inc(g_load[k], 16)

        with nc.Block() as block:
            @block.sync
            def _(sp):
                for m in range(4):
                    load_half(sp, m, m)

            @block.vector
            def _(dve):
                step = [0]

                def chained(ins):
                    step[0] += 1
                    ins.then_inc(f_v, 1)
                    dve.wait_ge(f_v, step[0])

                nc.vector.tensor_copy(ghh, bank[7][:, 0:128])
                nc.vector.tensor_copy(sums[:, 0:1], bank[7][:, 128:129])
                nc.vector.tensor_scalar(gah, bank[6][:, 0:128], 2.0, None, ALU.mult)
                nc.vector.tensor_copy(gaa, bank[6][:, 128:256])
                nc.vector.tensor_copy(sums[:, 1:2], bank[6][:, 256:257]).then_inc(f_b, 1)
                dve.wait_ge(f_p, 1)
                nc.vector.tensor_tensor(q1, bank[0][:, 0:128], w2a[:, :], ALU.mult)
                nc.vector.tensor_tensor(q2, bank[0][:, 128:256], w2b[:, :], ALU.mult).then_inc(f_b, 1)
                dve.wait_ge(f_p, 2)
                chained(nc.vector.tensor_scalar(bn[:, 8:10], bank[1][:, 0:2], 1.0 / N, None, ALU.mult))
                nc.vector.tensor_tensor(bn[:, 13:14], bn[:, 8:9], cols[:, B2:B2 + 1], ALU.add)
                chained(nc.vector.tensor_tensor(bn[:, 12:13], bn[:, 8:9], bn[:, 8:9], ALU.mult))
                nc.vector.tensor_tensor(bn[:, 10:11], bn[:, 9:10], bn[:, 12:13], ALU.subtract).then_inc(f_b, 1)
                dve.wait_ge(f_a, 1)
                chained(nc.vector.reciprocal(bn[:, 11:12], bn[:, 14:15]))
                nc.vector.tensor_tensor(bn[:, 12:13], cols[:, B2:B2 + 1], bn[:, 13:14], ALU.subtract)
                chained(nc.vector.tensor_tensor(bn[:, S2:S2 + 1], bn[:, 11:12], cols[:, G2:G2 + 1], ALU.mult))
                chained(nc.vector.scalar_tensor_tensor(bn[:, T2:T2 + 1], bn[:, 12:13], bn[:, S2:S2 + 1],
                                                       cols[:, BE2:BE2 + 1], ALU.mult, ALU.add))
                chained(nc.vector.tensor_scalar(bn[:, T2P:T2P + 1], bn[:, T2:T2 + 1], 1.0, None, ALU.add))
                nc.vector.tensor_scalar(dS, ident[:, :], bn[:, S2:S2 + 1], None, ALU.mult)
                nc.vector.tensor_scalar(dT, ident[:, :], bn[:, T2P:T2P + 1], None, ALU.mult).then_inc(f_b, 1)
                dve.wait_ge(f_p, 3)
                nc.vector.tensor_tensor(w2s[:, :], w2a[:, :], bank[2][:, 0:128], ALU.mult)
                nc.vector.tensor_copy(tB, bank[2][:, 128:256])
                chained(nc.vector.tensor_copy(hi_b, bank[2][:, 128:256]))
                chained(nc.vector.tensor_tensor(r1, tB, hi_b, ALU.subtract))
                chained(nc.vector.tensor_copy(mid_b, r1))
                chained(nc.vector.tensor_tensor(r2, r1, mid_b, ALU.subtract))
                chained(nc.vector.tensor_copy(lo_b, r2))
                for p, part in ((0, hi_b), (32, mid_b), (64, lo_b)):
                    for g in range(4):
                        last = nc.vector.tensor_copy(shift[p:p + 1, g * 128:(g + 1) * 128], part[p:p + 1, :])
                chained(last)

            @block.scalar
            def _(act):
                act.wait_ge(f_b, 3)
                nc.scalar.activation(bn[:, 14:15], bn[:, 10:11], ACT.Sqrt, bias=epsc[:, 1:2]).then_inc(f_a, 1)

            @block.tensor
            def _(pe):
                pe.wait_ge(f_b, 1)
                nc.tensor.matmul(bank[0][:, 0:128], ghh, w2a[:, :], start=True, stop=False)
                nc.tensor.matmul(bank[0][:, 0:128], gah, w2b[:, :], start=False, stop=True)
                nc.tensor.matmul(bank[0][:, 128:256], gaa, w2b[:, :], start=True, stop=True).then_inc(f_p, 1)
                nc.tensor.matmul(bank[1][:, 0:1], w2a[:, :], sums[:, 0:1], start=True, stop=False)
                nc.tensor.matmul(bank[1][:, 0:1], w2b[:, :], sums[:, 1:2], start=False, stop=True)
                pe.wait_ge(f_b, 2)
                nc.tensor.matmul(bank[1][:, 1:2], q1, ones[:, 0:1], start=True, stop=False)
                nc.tensor.matmul(bank[1][:, 1:2], q2, ones[:, 0:1], start=False, stop=True).then_inc(f_p, 1)
                pe.wait_ge(f_b, 4)
                nc.tensor.matmul(bank[2][:, 0:128], ones[:, :], dS, start=True, stop=True)
                nc.tensor.matmul(bank[2][:, 128:256], ones[:, :], dT, start=True, stop=True).then_inc(f_p, 1)

        g_store = [sem(f"g_store{k}") for k in range(4)]
        g_norm, g_relu, g_xp, g_tr, g_ht, g_y, g_exp, g_elu, g_sum = (
            sem("g_" + n) for n in ("norm", "relu", "xp", "tr", "ht", "y", "exp", "elu", "sum"))

        def group(n, back=0):
            return n + (9 - back)

        def own(k):
            return 2 if k % 4 else 3

        with nc.Block() as block:
            hT, xe = ([buf[q + b] for b in range(4)] for q in (0, 4))
            wv = [buf[8 + b] for b in range(2)]
            pT, pY = ([bank[q + b] for b in range(4)] for q in (0, 4))

            @block.sync
            def _(sp):
                def load(m, k):
                    if isinstance(m, int) and m < 4:
                        return
                    sp.wait_ge(g_norm, 2 * m + 2)
                    sp.wait_ge(g_relu, 2 * m + 2)
                    sp.wait_ge(g_xp, 2 * m + 2)
                    load_half(sp, m, k)

                def keep(m, k):
                    sp.wait_ge(g_sum, 2 * m + 10)
                    first = DUP if isinstance(m, int) and m >= 2 * NCH - 2 else 0
                    sp.dma_start(nodes(out, m, k, first), half(xp, k, first)).then_inc(g_store[k], 16)
                pipelined(sp, 2 * NCH, [(0, load), (5, keep)])
                for k in range(4):
                    sp.wait_ge(g_store[k], 16 * ((2 * NCH + 3 - k) // 4))

            @block.gpsimd
            def _(pool):
                pool.sem_inc(g_xp, 8)

                def add_bias(m, k):
                    pool.wait_ge(g_load[k], loaded(m, k))
                    wait_stored(pool, g_store[k], m, k)
                    nc.gpsimd.tensor_tensor(half(xp, k), half(xa, k),
                                            bom[:, :].unsqueeze(1).to_broadcast([128, T // 2, 128]), ALU.add).then_inc(g_xp, 2)
                pipelined(pool, 2 * NCH, [(0, add_bias)])

            @block.vector
            def _(dve):
                for q in (g_norm, g_elu, g_sum):
                    dve.sem_inc(q, 8)

                def normalize(n, k):
                    s, g = k // GR, k % GR
                    dve.wait_ge(g_load[k // 2], 2 * (n - k) + 16)
                    dve.wait_ge(g_tr, group(n, 8))
                    for t in range(own(k)):
                        last = nc.vector.tensor_scalar(hn[s][:, 4 * g + t, 0:128], xa[s][:, 4 * g + t, :],
                                                       rstd[:, ds(4 * n + t, 1)], nmr[:, ds(4 * n + t, 1)], ALU.mult, ALU.add)
                    last.then_inc(g_norm, 1)

                def combine(n, k):
                    s, g, b = k // GR, k % GR, k % 4
                    dve.wait_ge(g_exp, group(n))
                    dve.wait_ge(g_sum, group(n, 2))
                    nc.vector.scalar_tensor_tensor(wv[k % 2][:, :], xe[b][:, :], 1.0, pY[b][:, :], ALU.min, ALU.max).then_inc(g_elu, 1)

                def add(n, k):
                    s, g = k // GR, k % GR
                    dve.wait_ge(g_elu, group(n))
                    dve.wait_ge(g_xp, group(n + (1 - g % 2)))
                    o = xp[s][:, g * 4:(g + 1) * 4, :].rearrange("p t f -> p (t f)")
                    nc.vector.tensor_tensor(o, wv[k % 2][:, :], o, ALU.add).then_inc(g_sum, 1)
                pipelined(dve, NCH * GR, [(0, normalize), (5, combine), (6, add)], turn=2 * GR)

            @block.scalar
            def _(act):
                for q in (g_relu, g_ht, g_exp):
                    act.sem_inc(q, 8)

                def normalize(n, k):
                    s, g = k // GR, k % GR
                    act.wait_ge(g_load[k // 2], 2 * (n - k) + 16)
                    act.wait_ge(g_tr, group(n, 8))
                    for t in range(own(k), 4):
                        last = nc.scalar.activation(hn[s][:, 4 * g + t, 0:128], xa[s][:, 4 * g + t, :], ACT.Relu,
                                                    scale=rstd[:, ds(4 * n + t, 1)], bias=nmr[:, ds(4 * n + t, 1)])
                    last.then_inc(g_relu, 1)

                def relu(n, k):
                    b = k % 4
                    act.wait_ge(g_tr, group(n))
                    act.wait_ge(g_y, group(n, 4))
                    nc.scalar.activation(hT[b][:, :], pT[b][:, :], ACT.Relu).then_inc(g_ht, 1)

                def exp(n, k):
                    b = k % 4
                    act.wait_ge(g_y, group(n))
                    act.wait_ge(g_elu, group(n, 4))
                    nc.scalar.activation(xe[b][:, :], pY[b][:, :], ACT.Exp, bias=epsc[:, 2:3]).then_inc(g_exp, 1)
                pipelined(act, NCH * GR, [(0, normalize), (1, relu), (3, exp)], turn=2 * GR)

            @block.tensor
            def _(pe):
                for q in (g_tr, g_y):
                    pe.sem_inc(q, 8)

                def transpose(n, k):
                    b, s, g = k % 4, k // GR, k % GR
                    pe.wait_ge(g_norm, group(n))
                    pe.wait_ge(g_relu, group(n))
                    pe.wait_ge(g_ht, group(n, 4))
                    for t in range(4):
                        last = nc.tensor.transpose(pT[b][:, t * 128:(t + 1) * 128], hn[s][:, 4 * g + t, 0:128], ident[:, :])
                    last.then_inc(g_tr, 1)

                def project(n, k):
                    b = k % 4
                    pe.wait_ge(g_elu, group(n, 4))
                    nc.tensor.matmul(pY[b][:, :], ones_b[:, :], shift[:, :], start=True, stop=False)
                    pe.wait_ge(g_ht, group(n))
                    for t in range(4):
                        last = nc.tensor.matmul(pY[b][:, t * 128:(t + 1) * 128], hT[b][:, t * 128:(t + 1) * 128], w2s[:, :],
                                                start=False, stop=t == 3)
                    last.then_inc(g_y, 1)
                pipelined(pe, NCH * GR, [(1, transpose), (3, project)], turn=2 * GR)

        earlier = len(held)
        h_xd, h_keep, h_scat, h_qst = ([sem(f"h_{n}{k}") for k in range(4)] for n in ("xd", "keep", "scat", "qst"))
        h_exp, h_z, h_idx, h_cut, h_sums, h_sq, h_var, h_std, h_rs = (
            sem("h_" + n) for n in ("exp", "z", "idx", "cut", "sums", "sq", "var", "std", "rs"))
        h_elu, h_tr, h_x1, h_o, h_norm, h_back, h_ht, h_q, h_put = (
            sem("h_" + n) for n in ("elu", "tr", "x1", "o", "norm", "back", "ht", "q", "put"))

        def puts(pool, rows, ready, idx_sem, scat_sems):
            def waits(c, k):
                ready(c, k)
                pool.wait_ge(idx_sem, c + 1)

            def copy_indices(c, k):
                wait_stored(pool, scat_sems[k], c, k, TE)
                nc.gpsimd.tensor_copy(idx[k][:, :], scai[:, ds(c * TE, TE)]).then_inc(idx_sem, 1)

            def transfers(c, k):
                for t in range(TE):
                    nc.gpsimd.indirect_dma_start(out[:, :], bass.IndirectOffsetOnAxis(ap=idx[k][:, t:t + 1], axis=0),
                                                 rows[k][:, t, :], None, bounds_check=N - 1, oob_is_err=False
                                                 ).then_inc(scat_sems[k], 16)
            return waits, copy_indices, transfers

        with nc.Block() as block:
            xe, z, hT = ([b[:, 0:CE] for b in buf[q:q + 2]] for q in (0, 2, 4))
            hd = [tiles(b) for b in buf[6:8]]
            qo = [b[:, 0:CE] for b in buf[8:12]]
            xd, x1, ob = ([tiles(b) for b in spare[q:q + 4]] for q in (0, 4, 8))
            pX, pT, pQ = (bank[q:q + 2] for q in (0, 2, 4))

            @block.sync
            def _(sp):
                def load(c, k):
                    sp.wait_ge(h_tr, nth(c, 4))
                    sp.dma_start(xd[k], edge_rows(xd_d, c)).then_inc(h_xd[k], 16)

                def keep_rows(c, k):
                    sp.wait_ge(h_o, nth(c))
                    sp.dma_start(edge_rows(x1_d, c), ob[k]).then_inc(h_keep[k], 16)

                def keep_queries(c, k):
                    sp.wait_ge(h_put, nth(c))
                    sp.dma_start(q_d[ds(c, 1), :, :].rearrange("o p e -> p (o e)"), qo[k]).then_inc(h_qst[k], 16)
                pipelined(sp, ECH, [(0, load), (4, keep_rows), (10, keep_queries)])
                for k in range(4):
                    sp.wait_ge(h_keep[k], 16 * in_slot(k))
                    sp.wait_ge(h_qst[k], 16 * in_slot(k))

            @block.scalar
            def _(act):
                for q in (h_x1, h_ht, h_put):
                    act.sem_inc(q, 4)

                def exp(c, k):
                    act.wait_ge(h_elu, nth(c, 2))
                    nc.scalar.activation(xe[k % 2], chunk(c), ACT.Exp, scale=bn[:, S2:S2 + 1], bias=bn[:, T2:T2 + 1]).then_inc(h_exp, 1)

                def rows(c, k):
                    act.wait_ge(h_tr, nth(c))
                    act.wait_ge(h_norm, nth(c, 4))
                    act.wait_ge(h_o, nth(c, 4))
                    nc.scalar.copy(x1[k], pX[k % 2][0:TP, :].rearrange("p (t f) -> p t f", t=TE)).then_inc(h_x1, 1)

                def std(c, k):
                    if k % 2:
                        act.wait_ge(h_var, c + 1)
                        stddev(k - 1, TP, TE)
                        stddev(k, TP, TE).then_inc(h_std, 2)

                def relu(c, k):
                    act.wait_ge(h_back, nth(c))
                    act.wait_ge(h_q, nth(c, 2))
                    nc.scalar.activation(hT[k % 2], pT[k % 2][:, 0:CE], ACT.Relu).then_inc(h_ht, 1)

                def put(c, k):
                    act.wait_ge(h_q, nth(c))
                    wait_stored(act, h_qst[k], c, k)
                    nc.scalar.activation(qo[k], pQ[k % 2][:, 0:CE], ACT.Identity, bias=cols[:, BQ:BQ + 1]).then_inc(h_put, 1)
                pipelined(act, ECH, [(0, exp), (2, rows), (7, relu), (9, put), (3, std)])

            @block.tensor
            def _(pe):
                for q in (h_tr, h_back, h_q):
                    pe.sem_inc(q, 4)

                def transpose(c, k):
                    s = k % 2
                    pe.wait_ge(h_elu, nth(c))
                    pe.wait_ge(h_x1, nth(c, 2))
                    pe.wait_ge(h_xd[k], loaded(c, k))
                    for t in range(TE):
                        into = pX[s][0:TP, t * 128:(t + 1) * 128]
                        nc.tensor.matmul(into, z[s][:, t * TP:(t + 1) * TP], ident[:, :], start=True, stop=False)
                        last = nc.tensor.matmul(into, ident[0:TP, 0:TP], xd[k][:, t, :], start=False, stop=True)
                    last.then_inc(h_tr, 1)

                def back(c, k):
                    s = k % 2
                    pe.wait_ge(h_norm, nth(c))
                    pe.wait_ge(h_ht, nth(c, 2))
                    for t in range(TE):
                        last = nc.tensor.transpose(pT[s][:, t * TP:(t + 1) * TP], hd[s][:, t, :], ident[0:TP, 0:TP])
                    last.then_inc(h_back, 1)

                def project(c, k):
                    s = k % 2
                    pe.wait_ge(h_ht, nth(c))
                    pe.wait_ge(h_put, nth(c, 2))
                    nc.tensor.matmul(pQ[s][:, 0:CE], wqT[:, :], hT[s], start=True, stop=True).then_inc(h_q, 1)
                pipelined(pe, ECH, [(1, transpose), (6, back), (8, project)])

            @block.vector
            def _(dve):
                for q in (h_elu, h_o, h_norm):
                    dve.sem_inc(q, 4)

                def affine(c, k):
                    dve.wait_ge(h_tr, nth(c, 2))
                    nc.vector.tensor_scalar(z[k % 2], chunk(c), bn[:, S2:S2 + 1], bn[:, T2P:T2P + 1],
                                            ALU.mult, ALU.add).then_inc(h_z, 1)

                def elu(c, k):
                    s = k % 2
                    dve.wait_ge(h_z, c + 1)
                    dve.wait_ge(h_exp, c + 1)
                    nc.vector.scalar_tensor_tensor(z[s], xe[s], 1.0, z[s], ALU.min, ALU.max).then_inc(h_elu, 1)

                def stats(c, k):
                    dve.wait_ge(h_x1, nth(c))
                    for t in range(TE):
                        last = nc.vector.bn_stats(st[k][0:TP, t, :], x1[k][:, t, :])
                    last.then_inc(h_cut, 1)

                def add_bias(c, k):
                    wait_stored(dve, h_scat[k], c, k, TE)
                    wait_stored(dve, h_keep[k], c, k)
                    dve.wait_ge(h_x1, nth(c))
                    nc.vector.tensor_tensor(ob[k], x1[k], bom[0:TP, :].unsqueeze(1).to_broadcast([TP, TE, 128]),
                                            ALU.add).then_inc(h_o, 1)

                def invert(c, k):
                    dve.wait_ge(h_std, c + 1)
                    nc.vector.reciprocal(ln[k][0:TP, RS, 0:TE], ln[k][0:TP, STD, 0:TE]).then_inc(h_rs, 1)

                def normalize(c, k):
                    s = k % 2
                    dve.wait_ge(h_rs, c + 1)
                    dve.wait_ge(h_back, nth(c, 2))
                    for t in range(TE):
                        last = nc.vector.tensor_scalar(hd[s][:, t, :], x1[k][:, t, :], lnm[k][0:TP, t:t + 1],
                                                       ln[k][0:TP, RS, t:t + 1], ALU.subtract, ALU.mult)
                    last.then_inc(h_norm, 1)
                add_halves, square, variance = moments(dve, TP, TE, lambda k: k, lambda c: dve.wait_ge(h_cut, c + 1),
                                                       h_sums, h_sq, h_var)
                pipelined(dve, ECH, [(1, affine), (3, stats), (1, elu), (3, add_halves), (5, invert), (3, square),
                                     (3, add_bias), (3, variance), (5, normalize)])

            @block.gpsimd
            def _(pool):
                release(earlier)
                def ready(c, k):
                    pool.wait_ge(h_o, nth(c))
                indexed(pool, ECH, *puts(pool, ob, ready, h_idx, h_scat))
                for k in range(4):
                    pool.wait_ge(h_scat[k], 16 * TE * in_slot(k))

        k_load, k_q, k_cont, k_sst, k_mst = ([sem(f"k_{n}{k}") for k in range(4)] for n in ("load", "q", "cont", "sst", "mst"))
        k_idx, k_sub, k_cut, k_sums, k_sq, k_var, k_std, k_rs, k_first = (
            sem("k_" + n) for n in ("idx", "sub", "cut", "sums", "sq", "var", "std", "rs", "first"))
        k_norm, k_tr, k_put, k_k, k_kq, k_s, k_sput, k_mark, k_nb, k_max, k_edge = (
            sem("k_" + n) for n in ("norm", "tr", "put", "k", "kq", "s", "sput", "mark", "nb", "max", "edge"))

        def mark_load(sp, c, to, sema):
            sp.dma_start(to, cont_d[ds(c * CE, CE)].rearrange("(o e) -> o e", o=1)).then_inc(sema, 16)

        def whole(a, c):
            return a[ds(c, 1), :, :].rearrange("o p e -> p (o e)")

        with nc.Block() as block:
            gx = [tiles(b) for b in spare[0:4]]
            qs, sc = ([b[:, 0:CE] for b in q] for q in (spare[4:8], buf[4:8]))
            cont = [b[0:1, 0:CE // 2].bitcast(bf16) for b in buf[0:4]]
            nb, kq = ([b[:, 0:CE] for b in buf[q:q + 2]] for q in (8, 10))
            mx = [b[:, 0:CE + 1] for b in spare[16:20]]
            pT, pK, pS, pC = (bank[q:q + 2] for q in (0, 2, 4, 6))

            @block.gpsimd
            def _(pool):
                def free(c, k):
                    pool.wait_ge(k_tr, nth(c, 4))
                indexed(pool, ECH, *fetches(pool, srci, out, gx, free, k_idx, k_load))

            @block.sync
            def _(sp):
                def load(c, k):
                    sp.wait_ge(k_kq, nth(c, 4))
                    sp.dma_start(qs[k], whole(q_d, c)).then_inc(k_q[k], 16)
                    sp.wait_ge(k_mark, nth(c, 4))
                    mark_load(sp, c, cont[k], k_cont[k])

                def keep(c, k):
                    sp.wait_ge(k_sput, nth(c))
                    sp.dma_start(whole(s_d, c), sc[k]).then_inc(k_sst[k], 16)
                    sp.wait_ge(k_max, nth(c))
                    sp.wait_ge(k_edge, nth(c))
                    sp.dma_start(whole(m_d, c), mx[k]).then_inc(k_mst[k], 16)
                pipelined(sp, ECH, [(0, load), (7, keep)])
                for k in range(4):
                    sp.wait_ge(k_sst[k], 16 * in_slot(k))
                    sp.wait_ge(k_mst[k], 16 * in_slot(k))

            @block.vector
            def _(dve):
                for q in (k_norm, k_kq, k_max):
                    dve.sem_inc(q, 4)
                nc.vector.memset(mx[3], 0.0).then_inc(k_first, 1)
                dve.wait_ge(k_first, 1)

                def without_bias(c, k):
                    dve.wait_ge(k_load[k], loaded(c, k, TE))
                    nc.vector.tensor_tensor(gx[k], gx[k], bob[0:TP, :].unsqueeze(1).to_broadcast([TP, TE, 128]),
                                            ALU.subtract).then_inc(k_sub, 1)

                def stats(c, k):
                    s = k % 2
                    dve.wait_ge(k_sub, c + 1)
                    for t in range(TE):
                        last = nc.vector.bn_stats(st[s][0:TP, t, :], gx[k][:, t, :])
                    last.then_inc(k_cut, 1)

                def invert(c, k):
                    s = k % 2
                    dve.wait_ge(k_std, c + 1)
                    nc.vector.reciprocal(ln[s][0:TP, RS, 0:TE], ln[s][0:TP, STD, 0:TE]).then_inc(k_rs, 1)

                def normalize(c, k):
                    s = k % 2
                    dve.wait_ge(k_rs, c + 1)
                    for t in range(TE):
                        last = nc.vector.tensor_scalar(gx[k][:, t, :], gx[k][:, t, :], lnm[s][0:TP, t:t + 1],
                                                       ln[s][0:TP, RS, t:t + 1], ALU.subtract, ALU.mult)
                    last.then_inc(k_norm, 1)

                def times(c, k):
                    s = k % 2
                    dve.wait_ge(k_k, nth(c))
                    dve.wait_ge(k_q[k], loaded(c, k))
                    dve.wait_ge(k_s, nth(c, 2))
                    nc.vector.scalar_tensor_tensor(kq[s], pK[s][:, 0:CE], cols[:, BK:BK + 1], qs[k], ALU.add, ALU.mult).then_inc(k_kq, 1)

                def maximum(c, k):
                    s = k % 2
                    dve.wait_ge(k_sput, nth(c))
                    dve.wait_ge(k_nb, nth(c))
                    dve.wait_ge(k_max, nth(c, 1))
                    wait_stored(dve, k_mst[k], c, k)
                    nc.vector.tensor_tensor_scan(mx[k][:, 1:CE + 1], nb[s], sc[k], mx[(k - 1) % 4][:, CE:CE + 1],
                                                 ALU.add, ALU.max).then_inc(k_max, 1)
                add_halves, square, variance = moments(dve, TP, TE, lambda k: k % 2, lambda c: dve.wait_ge(k_cut, c + 1),
                                                       k_sums, k_sq, k_var)
                pipelined(dve, ECH, [(0, without_bias), (1, invert), (0, stats), (1, normalize), (0, add_halves), (5, times),
                                     (0, square), (8, maximum), (0, variance)])

            @block.tensor
            def _(pe):
                for q in (k_tr, k_k, k_s, k_mark):
                    pe.sem_inc(q, 4)

                def transpose(c, k):
                    pe.wait_ge(k_norm, nth(c))
                    pe.wait_ge(k_put, nth(c, 2))
                    for t in range(TE):
                        last = nc.tensor.transpose(pT[k % 2][:, t * TP:(t + 1) * TP], gx[k][:, t, :], ident[0:TP, 0:TP])
                    last.then_inc(k_tr, 1)

                def keys(c, k):
                    pe.wait_ge(k_put, nth(c))
                    pe.wait_ge(k_kq, nth(c, 2))
                    nc.tensor.matmul(pK[k % 2][:, 0:CE], wkT[:, :], chunk(c), start=True, stop=True).then_inc(k_k, 1)

                def scores(c, k):
                    pe.wait_ge(k_kq, nth(c))
                    pe.wait_ge(k_sput, nth(c, 2))
                    nc.tensor.matmul(pS[k % 2][:, 0:CE], blk[:, :], kq[k % 2], start=True, stop=True).then_inc(k_s, 1)

                def marks(c, k):
                    pe.wait_ge(k_cont[k], loaded(c, k))
                    pe.wait_ge(k_nb, nth(c, 2))
                    nc.tensor.matmul(pC[k % 2][:, 0:CE], ones_b[0:1, :], cont[k], start=True, stop=True).then_inc(k_mark, 1)
                pipelined(pe, ECH, [(2, transpose), (4, keys), (6, scores), (6, marks)])

            @block.scalar
            def _(act):
                for q in (k_put, k_sput, k_nb, k_edge):
                    act.sem_inc(q, 4)

                def std(c, k):
                    act.wait_ge(k_var, c + 1)
                    stddev(k % 2, TP, TE).then_inc(k_std, 1)

                def put(c, k):
                    act.wait_ge(k_tr, nth(c))
                    nc.scalar.activation(chunk(c), pT[k % 2][:, 0:CE], ACT.Relu).then_inc(k_put, 1)

                def starts(c, k):
                    act.wait_ge(k_mark, nth(c))
                    act.wait_ge(k_max, nth(c, 2))
                    nc.scalar.activation(nb[k % 2], pC[k % 2][:, 0:CE], ACT.Identity, scale=BIG, bias=epsc[:, 3:4]).then_inc(k_nb, 1)

                def put_scores(c, k):
                    act.wait_ge(k_s, nth(c))
                    act.wait_ge(k_max, nth(c, 4))
                    wait_stored(act, k_sst[k], c, k)
                    nc.scalar.copy(sc[k], pS[k % 2][:, 0:CE]).then_inc(k_sput, 1)

                def edge(c, k):
                    act.wait_ge(k_max, nth(c, 1))
                    wait_stored(act, k_mst[k], c, k)
                    nc.scalar.copy(mx[k][:, 0:1], mx[(k - 1) % 4][:, CE:CE + 1]).then_inc(k_edge, 1)
                pipelined(act, ECH, [(7, starts), (3, put), (7, put_scores), (9, edge), (0, std)])

        i_s, i_mx, i_x1, i_cont, i_scat = ([sem(f"i_{n}{k}") for k in range(4)] for n in ("s", "mx", "x1", "cont", "scat"))
        i_idx, i_first = sem("i_idx"), sem("i_first")
        i_v, i_diff, i_exp, i_w, i_sum, i_ones, i_den, i_rec, i_wide, i_rep, i_attn, i_o, i_out = (
            sem("i_" + n) for n in ("v", "diff", "exp", "w", "sum", "ones", "den", "rec",
                                    "wide", "rep", "attn", "o", "out"))

        with nc.Block() as block:
            fin, x1 = ([tiles(b) for b in q] for q in (buf[0:4], buf[4:8]))
            oo, ee = ([b[:, 0:CE] for b in q] for q in (spare[0:4], spare[4:8]))
            cont = [b[0:1, 0:CE // 2].bitcast(bf16) for b in buf[8:12]]
            mx = [b[:, 0:CE + 1] for b in spare[16:20]]
            dd, ll, aa = ([b[:, 0:CE] for b in spare[q:q + 2]] for q in (8, 10, 12))
            wv = [b[:, 0:CE] for b in buf[12:14]]
            rec = [b[:, 0, 0:TE * H].rearrange("p (t h) -> p t h", t=TE) for b in gram]
            wide = [tiles(b) for b in spare[22:24]]
            pick = ident[:, :].rearrange("p (h d) -> p h d", h=H)[:, :, 0]
            pV, pR, pO, pC = bank[0:2], bank[3], bank[4:6], bank[6:8]
            pL = bank[2][0:TP, 0:TE * H].rearrange("p (t h) -> p t h", t=TE)

            @block.sync
            def _(sp):
                def load(c, k):
                    sp.wait_ge(i_sum, nth(c, 4))
                    sp.dma_start(ee[k], whole(s_d, c)).then_inc(i_s[k], 16)
                    sp.dma_start(mx[k], whole(m_d, c)).then_inc(i_mx[k], 16)
                    mark_load(sp, c, cont[k], i_cont[k])

                def load_rows(c, k):
                    sp.wait_ge(i_o, nth(c, 4))
                    sp.dma_start(x1[k], edge_rows(x1_d, c)).then_inc(i_x1[k], 16)
                pipelined(sp, ECH, [(0, load), (3, load_rows)])

            @block.gpsimd
            def _(pool):
                def ready(c, k):
                    pool.wait_ge(i_out, nth(c))
                indexed(pool, ECH, *puts(pool, fin, ready, i_idx, i_scat))
                for k in range(4):
                    pool.wait_ge(i_scat[k], 16 * TE * in_slot(k))

            @block.scalar
            def _(act):
                for q in (i_exp, i_wide, i_out):
                    act.sem_inc(q, 4)

                def exp(c, k):
                    act.wait_ge(i_diff, nth(c))
                    nc.scalar.activation(ee[k], ee[k], ACT.Exp)
                    nc.scalar.activation(dd[k % 2], dd[k % 2], ACT.Exp).then_inc(i_exp, 1)

                def widen(c, k):
                    act.wait_ge(i_rec, nth(c))
                    act.wait_ge(i_rep, nth(c, 2))
                    nc.scalar.copy(wide[k % 2].rearrange("p t (h d) -> p (t h) d", h=H),
                                   rec[k % 2].rearrange("p t h -> p (t h)").unsqueeze(2).to_broadcast([TP, TE * H, HD])
                                   ).then_inc(i_wide, 1)

                def put(c, k):
                    act.wait_ge(i_o, nth(c))
                    wait_stored(act, i_scat[k], c, k, TE)
                    nc.scalar.copy(fin[k], pO[k % 2][0:TP, :].rearrange("p (t f) -> p t f", t=TE)).then_inc(i_out, 1)
                pipelined(act, ECH, [(0, exp), (2, widen), (4, put)])

            @block.tensor
            def _(pe):
                for q in (i_v, i_ones, i_rep, i_o):
                    pe.sem_inc(q, 4)

                def values(c, k):
                    pe.wait_ge(i_w, nth(c, 2))
                    pe.wait_ge(i_cont[k], loaded(c, k))
                    nc.tensor.matmul(pC[k % 2][:, 0:CE], ones_b[0:1, :], cont[k], start=True, stop=True)
                    nc.tensor.matmul(pV[k % 2][:, 0:CE], wvT[:, :], chunk(c), start=True, stop=True).then_inc(i_v, 1)

                def denominators(c, k):
                    pe.wait_ge(i_sum, nth(c))
                    pe.wait_ge(i_den, nth(c, 1))
                    for t in range(TE):
                        last = nc.tensor.matmul(pL[:, t, :], ll[k % 2][:, t * TP:(t + 1) * TP], pick, start=True, stop=True)
                    last.then_inc(i_ones, 1)

                def replicate(c, k):
                    pe.wait_ge(i_wide, nth(c))
                    pe.wait_ge(i_attn, nth(c, 1))
                    for t in range(TE):
                        last = nc.tensor.transpose(pR[:, t * TP:(t + 1) * TP], wide[k % 2][:, t, :], ident[0:TP, 0:TP])
                    last.then_inc(i_rep, 1)

                def output(c, k):
                    pe.wait_ge(i_attn, nth(c))
                    pe.wait_ge(i_x1[k], loaded(c, k))
                    pe.wait_ge(i_out, nth(c, 2))
                    for t in range(TE):
                        into = pO[k % 2][0:TP, t * 128:(t + 1) * 128]
                        nc.tensor.matmul(into, aa[k % 2][:, t * TP:(t + 1) * TP], woT[:, :], start=True, stop=False)
                        last = nc.tensor.matmul(into, ident[0:TP, 0:TP], x1[k][:, t, :], start=False, stop=True)
                    last.then_inc(i_o, 1)
                pipelined(pe, ECH, [(1, values), (2, denominators), (3, replicate), (4, output)])

            @block.vector
            def _(dve):
                for q in (i_diff, i_w, i_sum, i_den, i_rec, i_attn):
                    dve.sem_inc(q, 4)
                nc.vector.memset(ll[1], 0.0)
                nc.vector.memset(oo[3], 0.0).then_inc(i_first, 1)
                dve.wait_ge(i_first, 1)

                def differences(c, k):
                    s = k % 2
                    dve.wait_ge(i_s[k], loaded(c, k))
                    dve.wait_ge(i_mx[k], loaded(c, k))
                    dve.wait_ge(i_sum, nth(c, 2))
                    nc.vector.tensor_tensor(ee[k], ee[k], mx[k][:, 1:CE + 1], ALU.subtract)
                    nc.vector.tensor_tensor(dd[s], mx[k][:, 0:CE], mx[k][:, 1:CE + 1], ALU.subtract).then_inc(i_diff, 1)

                def weigh(c, k):
                    s = k % 2
                    dve.wait_ge(i_exp, nth(c))
                    dve.wait_ge(i_v, nth(c))
                    dve.wait_ge(i_sum, nth(c, 1))
                    nc.vector.scalar_tensor_tensor(dd[s], dd[s], 1.0, pC[s][:, 0:CE], ALU.min, ALU.mult)
                    nc.vector.scalar_tensor_tensor(wv[s], pV[s][:, 0:CE], cols[:, BV:BV + 1], ee[k], ALU.add, ALU.mult).then_inc(i_w, 1)

                def accumulate(c, k):
                    s = k % 2
                    dve.wait_ge(i_w, nth(c))
                    dve.wait_ge(i_ones, nth(c, 2))
                    dve.wait_ge(i_attn, nth(c, 4))
                    nc.vector.tensor_tensor_scan(ll[s], dd[s], ee[k], ll[1 - s][:, CE - 1:CE], ALU.mult, ALU.add)
                    nc.vector.tensor_tensor_scan(oo[k], dd[s], wv[s], oo[(k - 1) % 4][:, CE - 1:CE], ALU.mult, ALU.add).then_inc(i_sum, 1)

                def guard(c, k):
                    dve.wait_ge(i_ones, nth(c))
                    dve.wait_ge(i_wide, nth(c, 2))
                    nc.vector.tensor_scalar(rec[k % 2], pL, SM_EPS, None, ALU.add).then_inc(i_den, 1)

                def invert(c, k):
                    s = k % 2
                    dve.wait_ge(i_den, nth(c))
                    nc.vector.reciprocal(rec[s], rec[s]).then_inc(i_rec, 1)

                def attend(c, k):
                    s = k % 2
                    dve.wait_ge(i_rep, nth(c))
                    dve.wait_ge(i_o, nth(c, 2))
                    nc.vector.tensor_tensor(aa[s], oo[k], pR[:, 0:CE], ALU.mult).then_inc(i_attn, 1)
                pipelined(dve, ECH, [(1, weigh), (0, differences), (2, guard), (1, accumulate), (2, invert), (3, attend)])



_INS = ["x", "src", "dst", "edge_attr_128", "L0_gnn_W1", "L0_gnn_b1", "L0_gnn_g1", "L0_gnn_be1", "L0_gnn_W2", "L0_gnn_b2",
        "L0_gnn_g2", "L0_gnn_be2", "L1_gnn_Wq", "L1_gnn_bq", "L1_gnn_Wk", "L1_gnn_bk", "L1_gnn_Wv", "L1_gnn_bv", "L1_gnn_Wo",
        "L1_gnn_bo"]


def kernel(**inputs):
    import numpy as np
    import concourse.bacc as bacc
    from concourse.bass_utils import run_bass_kernel_spmd

    nc = bacc.Bacc("TRN2", target_bir_lowering=False, num_devices=1)
    arrays, args = {}, []
    for name in _INS:
        a = np.ascontiguousarray(inputs[name])
        arrays[f"in_{name}"] = a
        args.append(nc.dram_tensor(f"in_{name}", a.shape, mybir.dt.from_np(a.dtype), kind="ExternalInput").ap())
    out = nc.dram_tensor("out_rows", (N, D), f32, kind="ExternalOutput").ap()
    program(nc, *args, out)
    r = run_bass_kernel_spmd(nc, [arrays], core_ids=[0])
    return r.results[0]["out_rows"]
```
